# Optimizing a Trainium2 kernel written in Bass

```python
import numpy as np
import jax
import jax.numpy as jnp

def _softmax(x, axis=-1):
    return jax.nn.softmax(x, axis=axis)

def _gelu(x):
    return jax.nn.gelu(x, approximate=True)

def _silu(x):
    return jax.nn.silu(x)

def _sigmoid(x):
    return jax.nn.sigmoid(x)

def _layernorm(x, axis=-1, eps=1e-05):
    m = jnp.mean(x, axis=axis, keepdims=True)
    v = jnp.var(x, axis=axis, keepdims=True)
    return (x - m) / jnp.sqrt(v + eps)

def _scatter_add(tgt, idx, src, axis=0):
    return tgt.at[idx].add(src)

def _segment_sum(src, seg, n):
    return jax.ops.segment_sum(src, seg, n)
kernel_name = 'mk_adj_resnorm_d4_adj_r2_817e0f'

def setup_inputs(seed: int=0):
    np.random.seed(seed)
    _w = jnp.asarray

    def _rec_inputs():
        import jax
        import jax.numpy as jnp
        _gk = jax.random.key(seed)
        x = -0.001003 + 1 * jax.random.normal(jax.random.fold_in(_gk, 1), (2048, 256), jnp.float32)
        _w = (1.0 + jnp.arange(2048, dtype=jnp.float32)) ** (-0.5)
        _w = _w / _w.mean()
        _pij = jnp.clip(0.0078125 * _w[:, None] * _w[None, :], 0.0, 1.0)
        _a = jax.random.uniform(jax.random.fold_in(_gk, 2), (2048, 2048)) < _pij
        _a = jnp.logical_or(_a, jnp.eye(2048, dtype=bool))
        _af = _a.astype(jnp.float32)
        adj = _af
        return (x, adj)
    x, adj = _rec_inputs()

    def _L0_gnn_setup():
        import jax, jax.numpy as jnp
        import numpy as np
        N, F, H = (1536, 256, 4)
        D = F // H
        ALPHA = 0.5
        EPS = 1e-06

        def _batchnorm(x, gamma, beta):
            m = jnp.mean(x, axis=0)
            v = jnp.var(x, axis=0)
            return (x - m) * jax.lax.rsqrt(v + EPS) * gamma + beta

        def _masked_softmax(scores, mask):
            s = jnp.where(mask, scores, -jnp.inf)
            att = jax.nn.softmax(s, axis=-1)
            return jnp.where(mask, att, 0.0)

        def _mlp_block(x, Wm, bm, g, b):
            h = jax.nn.elu(x @ Wm.T + bm) + x
            return _batchnorm(h, g, b)
        key = jax.random.key(seed)
        ks = jax.random.split(key, 12)
        X = jax.random.normal(ks[0], (N, F), dtype=jnp.float32)
        eye = jnp.eye(N, dtype=jnp.float32)
        local = (jax.random.uniform(ks[1], (N, N)) < 32.0 / N).astype(jnp.float32)
        local = jnp.clip(local + eye, 0.0, 1.0)
        longr = (jax.random.uniform(ks[2], (N, N)) < 16.0 / N).astype(jnp.float32)
        longr = jnp.clip(longr + eye, 0.0, 1.0)
        W = jax.random.normal(ks[3], (H, D, D), dtype=jnp.float32) * 0.1
        V = jax.random.normal(ks[4], (H, 2, D, 1), dtype=jnp.float32) * 0.1
        return {'X': X, 'local_pattern': local, 'long_range_pattern': longr, 'W': W, 'V': V, 'enc_bn_gamma': jnp.ones((F,), jnp.float32), 'enc_bn_beta': jnp.zeros((F,), jnp.float32), 'enc_mlp_W': jax.random.normal(ks[5], (F, F), dtype=jnp.float32) * 0.02, 'enc_mlp_b': jnp.zeros((F,), jnp.float32), 'enc_mlp_bn_gamma': jnp.ones((F,), jnp.float32), 'enc_mlp_bn_beta': jnp.zeros((F,), jnp.float32), 'dec_mlp_W': jax.random.normal(ks[6], (F, F), dtype=jnp.float32) * 0.02, 'dec_mlp_b': jnp.zeros((F,), jnp.float32), 'dec_mlp_bn_gamma': jnp.ones((F,), jnp.float32), 'dec_mlp_bn_beta': jnp.zeros((F,), jnp.float32)}
    _L0_gnn_all = _L0_gnn_setup()
    _L0_gnn_in = {k: v for k, v in _L0_gnn_all.items() if k in ('W', 'V', 'enc_bn_gamma', 'enc_bn_beta', 'enc_mlp_W', 'enc_mlp_b', 'enc_mlp_bn_gamma', 'enc_mlp_bn_beta', 'dec_mlp_W', 'dec_mlp_b', 'dec_mlp_bn_gamma', 'dec_mlp_bn_beta')}
    del _L0_gnn_all

    def _L1_gnn_setup():
        import jax, jax.numpy as jnp
        import numpy as np
        N = 4096
        DIN = 256
        DOUT = 256
        key = jax.random.key(seed)
        k1, k2, k3 = jax.random.split(key, 3)
        H_in = jax.random.normal(k1, (N, DIN), dtype=jnp.float32)
        u = jax.random.uniform(k2, (N, N), dtype=jnp.float32)
        upper = (u < 0.005).astype(jnp.float32)
        upper = jnp.triu(upper, k=1)
        A = upper + upper.T
        limit = np.sqrt(6.0 / (DIN + DOUT)).astype(np.float32)
        W = jax.random.uniform(k3, (DIN, DOUT), dtype=jnp.float32, minval=-limit, maxval=limit)
        return {'H_in': H_in, 'A': A, 'W': W}
    _L1_gnn_all = _L1_gnn_setup()
    _L1_gnn_in = {k: v for k, v in _L1_gnn_all.items() if k in ('W',)}
    del _L1_gnn_all

    def _L2_gnn_setup():
        import jax, jax.numpy as jnp
        import numpy as np
        N = 4096
        DIM_IN = 256
        DIM_Q = 256
        DIM_K = 256
        key = jax.random.key(seed)
        ks = jax.random.split(key, 9)
        s = 0.02
        return {'x': jax.random.normal(ks[0], (N, DIM_IN), dtype=jnp.float32), 'adj_matrix': jax.random.normal(ks[1], (N, N), dtype=jnp.float32), 'spatial_matrix': jax.random.normal(ks[2], (N, N), dtype=jnp.float32), 'Wq': jax.random.normal(ks[3], (DIM_IN, DIM_Q), dtype=jnp.float32) * s, 'bq': jax.random.normal(ks[4], (DIM_Q,), dtype=jnp.float32) * s, 'Wk': jax.random.normal(ks[5], (DIM_IN, DIM_K), dtype=jnp.float32) * s, 'bk': jax.random.normal(ks[6], (DIM_K,), dtype=jnp.float32) * s, 'Wv': jax.random.normal(ks[7], (DIM_IN, DIM_K), dtype=jnp.float32) * s, 'bv': jax.random.normal(ks[8], (DIM_K,), dtype=jnp.float32) * s}
    _L2_gnn_all = _L2_gnn_setup()
    _L2_gnn_in = {k: v for k, v in _L2_gnn_all.items() if k in ('Wq', 'bq', 'Wk', 'bk', 'Wv', 'bv')}
    del _L2_gnn_all

    def _L3_gnn_setup():
        import jax, jax.numpy as jnp
        import numpy as np
        EPS = 1e-08
        key = jax.random.key(seed)
        k1, k2, k3, k4 = jax.random.split(key, 4)
        N, IN, OUT = (4096, 256, 256)
        x = jax.random.normal(k1, (N, IN), dtype=jnp.float32)
        adj = jax.random.uniform(k2, (N, N), dtype=jnp.float32)
        W = jax.random.normal(k3, (OUT, IN), dtype=jnp.float32) * (1.0 / np.sqrt(IN))
        b = jax.random.normal(k4, (OUT,), dtype=jnp.float32) * 0.01
        return {'x': x, 'adj': adj, 'W': W, 'b': b}
    _L3_gnn_all = _L3_gnn_setup()
    _L3_gnn_in = {k: v for k, v in _L3_gnn_all.items() if k in ('W', 'b')}
    del _L3_gnn_all
    return {'x': x, 'adj': adj, 'L0_gnn_W': _L0_gnn_in['W'], 'L0_gnn_V': _L0_gnn_in['V'], 'L0_gnn_enc_bn_gamma': _L0_gnn_in['enc_bn_gamma'], 'L0_gnn_enc_bn_beta': _L0_gnn_in['enc_bn_beta'], 'L0_gnn_enc_mlp_W': _L0_gnn_in['enc_mlp_W'], 'L0_gnn_enc_mlp_b': _L0_gnn_in['enc_mlp_b'], 'L0_gnn_enc_mlp_bn_gamma': _L0_gnn_in['enc_mlp_bn_gamma'], 'L0_gnn_enc_mlp_bn_beta': _L0_gnn_in['enc_mlp_bn_beta'], 'L0_gnn_dec_mlp_W': _L0_gnn_in['dec_mlp_W'], 'L0_gnn_dec_mlp_b': _L0_gnn_in['dec_mlp_b'], 'L0_gnn_dec_mlp_bn_gamma': _L0_gnn_in['dec_mlp_bn_gamma'], 'L0_gnn_dec_mlp_bn_beta': _L0_gnn_in['dec_mlp_bn_beta'], 'L1_gnn_W': _L1_gnn_in['W'], 'L2_gnn_Wq': _L2_gnn_in['Wq'], 'L2_gnn_bq': _L2_gnn_in['bq'], 'L2_gnn_Wk': _L2_gnn_in['Wk'], 'L2_gnn_bk': _L2_gnn_in['bk'], 'L2_gnn_Wv': _L2_gnn_in['Wv'], 'L2_gnn_bv': _L2_gnn_in['bv'], 'L3_gnn_W': _L3_gnn_in['W'], 'L3_gnn_b': _L3_gnn_in['b']}

def reference(x, adj, L0_gnn_W, L0_gnn_V, L0_gnn_enc_bn_gamma, L0_gnn_enc_bn_beta, L0_gnn_enc_mlp_W, L0_gnn_enc_mlp_b, L0_gnn_enc_mlp_bn_gamma, L0_gnn_enc_mlp_bn_beta, L0_gnn_dec_mlp_W, L0_gnn_dec_mlp_b, L0_gnn_dec_mlp_bn_gamma, L0_gnn_dec_mlp_bn_beta, L1_gnn_W, L2_gnn_Wq, L2_gnn_bq, L2_gnn_Wk, L2_gnn_bk, L2_gnn_Wv, L2_gnn_bv, L3_gnn_W, L3_gnn_b):
    import jax
    import jax.numpy as jnp

    def _L0_gnn_ref(X, local_pattern, long_range_pattern, W, V, enc_bn_gamma, enc_bn_beta, enc_mlp_W, enc_mlp_b, enc_mlp_bn_gamma, enc_mlp_bn_beta, dec_mlp_W, dec_mlp_b, dec_mlp_bn_gamma, dec_mlp_bn_beta):
        import jax, jax.numpy as jnp
        import numpy as np
        N, F, H = (1536, 256, 4)
        D = F // H
        ALPHA = 0.5
        EPS = 1e-06

        def _batchnorm(x, gamma, beta):
            m = jnp.mean(x, axis=0)
            v = jnp.var(x, axis=0)
            return (x - m) * jax.lax.rsqrt(v + EPS) * gamma + beta

        def _masked_softmax(scores, mask):
            s = jnp.where(mask, scores, -jnp.inf)
            att = jax.nn.softmax(s, axis=-1)
            return jnp.where(mask, att, 0.0)

        def _mlp_block(x, Wm, bm, g, b):
            h = jax.nn.elu(x @ Wm.T + bm) + x
            return _batchnorm(h, g, b)
        n = X.shape[0]
        Xh = X.reshape(n, H, D).transpose(1, 0, 2)
        Xw = jnp.einsum('hnd,hde->hne', Xh, W)
        f1 = jnp.einsum('hnd,hd->hn', Xw, V[:, 0, :, 0])
        f2 = jnp.einsum('hnd,hd->hn', Xw, V[:, 1, :, 0])
        sig = jax.nn.sigmoid(f1[:, :, None] + f2[:, None, :])
        lmask = (local_pattern != 0)[None]
        gmask = (long_range_pattern != 0)[None]
        local_att = _masked_softmax(local_pattern[None] * sig, lmask)
        long_att = _masked_softmax(long_range_pattern[None] * sig, gmask)
        att = ALPHA * long_att + (1.0 - ALPHA) * local_att
        Xa = jnp.einsum('hij,hjd->hid', att, Xw)
        Xc = Xa.transpose(1, 0, 2).reshape(n, F)
        Xn = _batchnorm(Xc, enc_bn_gamma, enc_bn_beta)
        emb = _mlp_block(Xn, enc_mlp_W, enc_mlp_b, enc_mlp_bn_gamma, enc_mlp_bn_beta)
        Yh = emb.reshape(n, H, D).transpose(1, 0, 2)
        Y = jnp.einsum('hij,hjd->hid', att, Yh)
        Y = jnp.einsum('hnd,hed->hne', Y, W)
        Yc = Y.transpose(1, 0, 2).reshape(n, F)
        Yc = jax.nn.elu(Yc)
        out = _mlp_block(Yc, dec_mlp_W, dec_mlp_b, dec_mlp_bn_gamma, dec_mlp_bn_beta)
        return out

    def _L1_gnn_ref(H_in, A, W):
        import jax, jax.numpy as jnp
        import numpy as np
        N = 4096
        DIN = 256
        DOUT = 256
        A_ = A + jnp.eye(A.shape[0], dtype=A.dtype)
        d_inv_sqrt = jax.lax.rsqrt(A_.sum(axis=1))
        A_norm = A_ * d_inv_sqrt[:, None] * d_inv_sqrt[None, :]
        H_out = jnp.matmul(jnp.matmul(A_norm, H_in), W)
        return jax.nn.relu(H_out)

    def _L2_gnn_ref(x, adj_matrix, spatial_matrix, Wq, bq, Wk, bk, Wv, bv):
        import jax, jax.numpy as jnp
        import numpy as np
        N = 4096
        DIM_IN = 256
        DIM_Q = 256
        DIM_K = 256
        query = x @ Wq + bq
        key = x @ Wk + bk
        value = x @ Wv + bv
        scale = 1.0 / jnp.sqrt(jnp.asarray(query.shape[-1], dtype=query.dtype))
        a = query @ key.T * scale
        a = a + adj_matrix + spatial_matrix
        attn = jax.nn.softmax(a, axis=-1)
        return attn @ value

    def _L3_gnn_ref(x, adj, W, b):
        import jax, jax.numpy as jnp
        import numpy as np
        EPS = 1e-08
        deg = adj.sum(axis=1)
        dis = (deg + EPS) ** (-0.5)
        a_norm = dis[:, None] * adj * dis[None, :]
        h = a_norm @ x
        return h @ W.T + b
    x = _layernorm(x + _L0_gnn_ref(x, adj, adj, L0_gnn_W, L0_gnn_V, L0_gnn_enc_bn_gamma, L0_gnn_enc_bn_beta, L0_gnn_enc_mlp_W, L0_gnn_enc_mlp_b, L0_gnn_enc_mlp_bn_gamma, L0_gnn_enc_mlp_bn_beta, L0_gnn_dec_mlp_W, L0_gnn_dec_mlp_b, L0_gnn_dec_mlp_bn_gamma, L0_gnn_dec_mlp_bn_beta), axis=-1)
    x = _layernorm(x + _L1_gnn_ref(x, adj, L1_gnn_W), axis=-1)
    x = _layernorm(x + _L2_gnn_ref(x, adj, adj, L2_gnn_Wq, L2_gnn_bq, L2_gnn_Wk, L2_gnn_bk, L2_gnn_Wv, L2_gnn_bv), axis=-1)
    x = _layernorm(x + _L3_gnn_ref(x, adj, L3_gnn_W, L3_gnn_b), axis=-1)
    return x

_drawn_inputs = setup_inputs


def setup_inputs(seed=0):
    import zlib

    import numpy as np

    out = dict(_drawn_inputs(seed))
    spreads = {'L0_gnn_enc_bn_gamma': (1.0, 0.2),
     'L0_gnn_enc_bn_beta': (0.0, 2.0),
     'L0_gnn_enc_mlp_b': (0.0, 0.8),
     'L0_gnn_enc_mlp_bn_gamma': (1.0, 0.2),
     'L0_gnn_enc_mlp_bn_beta': (0.0, 0.423),
     'L0_gnn_dec_mlp_b': (0.0, 0.706),
     'L0_gnn_dec_mlp_bn_gamma': (1.0, 0.2),
     'L0_gnn_dec_mlp_bn_beta': (0.0, 0.1)}
    factors = {'L2_gnn_Wq': 8.0, 'L2_gnn_bq': 8.0, 'L2_gnn_Wk': 8.0, 'L2_gnn_bk': 64.0, 'L3_gnn_b': 6.589}
    for name, (base, spread) in spreads.items():
        noise = np.random.default_rng([zlib.crc32(name.encode()), seed]).standard_normal(out[name].shape)
        drawn = base * np.exp(spread * noise) if base else spread * noise
        out[name] = jnp.asarray(drawn.astype(out[name].dtype))
    for name, factor in factors.items():
        out[name] = (out[name] * factor).astype(out[name].dtype)
    return out
```

```python
from contextlib import ExitStack

import concourse.bass as bass
from concourse import mybir

ACT = mybir.ActivationFunctionType
ALU = mybir.AluOpType
AX = mybir.AxisListType
F32 = mybir.dt.float32
BF16 = mybir.dt.bfloat16

P = 128
N = 2048
F = 256
H = 4
D = F // H
NB = N // P
FB = F // P
CH = 512
NC = N // CH
BPC = CH // P
EPS_BN = 1e-6
EPS_LN = 1e-5
EPS_DEG = 1e-8
TINY = 1e-30
PER_BANK = 6
HEAD_BANKS = 3

W_ENC, W_DEC, W_L1, W_Q, W_K, W_V, W_L3 = range(7)
G_ENC, B_ENC, BIAS_ENC, G_ENC2, B_ENC2, BIAS_DEC, G_DEC, B_DEC, BIAS_Q, BIAS_K = range(10)


def gnn_stack(nc, x, xT, adjT, wbd, wtbd, v0rep, v1, weights, params, rows, out):
    with ExitStack() as ctx:
        def sb(name, shape, dt=F32):
            return ctx.enter_context(nc.sbuf_tensor(name, shape, dt))

        def sem(name):
            return ctx.enter_context(nc.semaphore(name))

        adj_t = sb("adj_t", [P, NB, N], BF16)
        f1_all = sb("f1_all", [P, H * N])
        big = sb("big", [P, 4 * N])
        node_b = sb("node_b", [P, NB * H * (D + 1)])
        node_a = sb("node_a", [P, NB * F])
        x_now = sb("x_now", [P, NB, F])
        w_all = sb("w_all", [P, 7, FB, F])
        wbd_s = sb("wbd_s", [P, FB, P])
        wtbd_s = sb("wtbd_s", [P, FB, P])
        v0_s = sb("v0_s", [P, H, P])
        v1_s = sb("v1_s", [P, FB, 2])
        par = sb("par", [P, 10, FB])
        row_s = sb("row_s", [P, 2, F])
        ident = sb("ident", [P, P])
        eye_b = sb("eye_b", [P, P], BF16)
        two_b = sb("two_b", [P, P], BF16)
        zeros_b = sb("zeros_b", [P, CH], BF16)
        ones_b = sb("ones_b", [P, 1], BF16)
        minus_half = sb("minus_half", [P, NB])
        f2_half = sb("f2_half", [P, NB, H])
        deg = sb("deg", [P, NB])
        deg1 = sb("deg1", [P, NB])
        deg3 = sb("deg3", [P, NB])
        dinv1 = sb("dinv1", [P, NB])
        dinv3 = sb("dinv3", [P, NB])
        sums = sb("sums", [P, 2, NB])
        rinv = sb("rinv", [P, H, NB])
        bn_st = sb("bn_st", [P, FB, NC, 6])
        bn_mv = sb("bn_mv", [P, FB, 2])
        bn_ve = sb("bn_ve", [P, FB])
        bn_rs = sb("bn_rs", [P, FB])
        bn_a = sb("bn_a", [P, FB])
        bn_t = sb("bn_t", [P, FB])
        bn_b = sb("bn_b", [P, FB])
        ln_st = sb("ln_st", [P, NB, 6])
        ln_mv = sb("ln_mv", [P, NB, 2])
        ln_ve = sb("ln_ve", [P, NB])
        ln_rs = sb("ln_rs", [P, NB])
        q_blk = sb("q_blk", [P, 2, FB, P])
        neg_max = sb("neg_max", [P, 2])
        row_sum = sb("row_sum", [P, NB])
        row_inv = sb("row_inv", [P, NB])

        feat_1 = big[:, 0:2 * N].rearrange("p (c n) -> p c n", c=FB)
        feat_2 = big[:, 2 * N:4 * N].rearrange("p (c n) -> p c n", c=FB)
        att = big[:, :].rearrange("p (k n) -> p k n", k=4)
        xw = node_b[:, :].rearrange("p (b h e) -> p b h e", b=NB, h=H)
        yh = node_b[:, 0:NB * F].rearrange("p (b f) -> p b f", b=NB)
        feat_3 = node_b[:, 0:NB * F].rearrange("p (c n) -> p c n", c=FB)
        e_tmp = node_b[:, 0:2 * CH].rearrange("p (k n) -> p k n", k=2)
        r_tmp = node_b[:, 2 * CH:4 * CH].rearrange("p (k n) -> p k n", k=2)
        nodes = node_a[:, :].rearrange("p (b f) -> p b f", b=NB)
        adj_row = node_a[:, :].rearrange("p (k n) -> p k n", k=2)
        f1 = f1_all[:, :].rearrange("p (h n) -> p h n", h=H)
        parts = big[:, 0:3 * NB * F // 2].bitcast(BF16).rearrange("p (s b f) -> p s b f", s=3, b=NB)
        prob = f1_all[:, 0:2 * N].rearrange("p (k n) -> p k n", k=2)
        prob_t = f1_all[:, 2 * N:4 * N].rearrange("p (k b i) -> p k b i", k=2, b=NB)

        ps = ctx.enter_context(nc.psum_tensor("ps", [P, 8, CH], F32))

        in_x = sem("in_x")
        in_w = sem("in_w")
        adj_in = [sem("adj_in0"), sem("adj_in1")]
        adj_cast = sem("adj_cast")
        consts = sem("consts")
        const_a = sem("const_a")
        full = {}
        kept = {}
        for st in ("xwT", "xw", "f1", "f2", "deg", "xcT", "enc", "emb", "yT", "yw", "dec", "l0",
                   "ax1", "z1", "x2T", "qk", "v", "ax3", "z3"):
            full[st] = sem("full_" + st)
            kept[st] = sem("kept_" + st)
        elu_e = sem("elu_e")
        elu_r = sem("elu_r")
        elu_free = sem("elu_free")
        elu_done = sem("elu_done")
        dve = sem("dve")
        tanh_done = sem("tanh_done")
        exp_done = sem("exp_done")
        mask_done = sem("mask_done")
        att_free = sem("att_free")
        acc_kept = sem("acc_kept")
        var_ready = sem("var_ready")
        rstd_ready = sem("rstd_ready")
        bn_done = sem("bn_done")
        ln_done = sem("ln_done")
        part_ready = sem("part_ready")
        q_ready = sem("q_ready")
        s_full = sem("s_full")
        max_ready = sem("max_ready")
        p_ready = sem("p_ready")
        t_full = sem("t_full")
        t_act = sem("t_act")
        t_dve = sem("t_dve")
        o_full = sem("o_full")
        o_kept = sem("o_kept")
        mean_inv = sem("mean_inv")
        out_done = sem("out_done")

        block = ctx.enter_context(nc.Block())

        @block.sync
        def _(sp):
            sp.dma_start(feat_1, xT.rearrange("(c p) n -> p c n", p=P)).then_inc(in_x, 16)
            sp.dma_start(wbd_s[:], wbd.rearrange("c p e -> p c e")).then_inc(in_x, 16)
            sp.dma_start(v0_s[:], v0rep.rearrange("h p e -> p h e")).then_inc(in_x, 16)
            sp.dma_start(v1_s[:], v1.rearrange("c p e -> p c e")).then_inc(in_x, 16)
            for s in range(2):
                sp.dma_start(adj_row[:, s, :], adjT[s * P:(s + 1) * P, :]).then_inc(adj_in[s], 16)
            with sp.Fori(1, NB // 2) as m:
                for s in range(2):
                    sp.wait_ge(adj_cast, 2 * m + s - 1)
                    sp.dma_start(adj_row[:, s, :], adjT[bass.ds((2 * m + s) * P, P), :]).then_inc(adj_in[s], 16)
            out_v = out.rearrange("(b p) f -> p b f", p=P)
            for g in range(4):
                sp.wait_ge(ln_done, 3 * NB + 4 * g + 4)
                sp.dma_start(out_v[:, 4 * g:4 * g + 4, :], x_now[:, 4 * g:4 * g + 4, :]).then_inc(out_done, 16)
            sp.wait_ge(out_done, 64)

        @block.gpsimd
        def _(pool):
            pool.memset(ident[:], 0.0).then_inc(const_a, 1)
            pool.memset(eye_b[:], 0.0).then_inc(const_a, 1)
            pool.memset(two_b[:], 0.0).then_inc(const_a, 1)
            pool.memset(zeros_b[:], 0.0).then_inc(consts, 1)
            pool.memset(ones_b[:], 1.0).then_inc(att_free, 4)
            pool.memset(minus_half[:], -0.5).then_inc(const_a, 1)
            pool.wait_ge(const_a, 4)
            for m, v in ((ident, 1.0), (eye_b, 1.0), (two_b, 2.0)):
                pool.affine_select(out=m[:], in_=m[:], compare_op=ALU.not_equal, fill=v, base=0,
                                   pattern=[[-1, P]], channel_multiplier=1).then_inc(consts, 1)
            with pool.Fori(0, NB // 2) as m:
                for s in range(2):
                    pool.wait_ge(adj_in[s], 16 * m + 16)
                    pool.tensor_copy(adj_t[:, bass.ds(2 * m + s, 1), :], adj_row[:, bass.ds(s, 1), :]).then_inc(adj_cast, 1)

            n = 0

            def power(dst, src, width):
                nonlocal n
                n += 1
                pool.wait_ge(var_ready, n)
                pool.tensor_tensor(dst, src, minus_half[:, 0:width], ALU.pow).then_inc(rstd_ready, 1)

            power(bn_rs[:], bn_ve[:], FB)
            power(bn_rs[:], bn_ve[:], FB)
            power(bn_rs[:], bn_ve[:], FB)
            power(dinv1[:], deg1[:], NB)
            power(dinv3[:], deg3[:], NB)
            power(ln_rs[:], ln_ve[:], NB)
            power(ln_rs[:], ln_ve[:], NB)

            pool.wait_ge(kept["qk"], 8)
            for b in range(2):
                pool.tensor_copy(q_blk[:, b], feat_2[:, :, b * P:(b + 1) * P]).then_inc(q_ready, 1)
            with pool.Fori(1, NB // 2) as m:
                for b in range(2):
                    pool.wait_ge(s_full, 2 * m + b - 1)
                    pool.tensor_copy(q_blk[:, b], feat_2[:, :, bass.ds((2 * m + b) * P, P)]).then_inc(q_ready, 1)

            power(ln_rs[:], ln_ve[:], NB)
            power(ln_rs[:], ln_ve[:], NB)

        @block.scalar
        def _(act):
            act.dma_start(par[:], params).then_inc(in_w, 16)
            act.dma_start(w_all[:], weights).then_inc(in_w, 16)
            act.dma_start(wtbd_s[:], wtbd.rearrange("c p e -> p c e")).then_inc(in_w, 16)
            act.dma_start(row_s[:], rows).then_inc(in_w, 16)
            act.dma_start(x_now[:], x.rearrange("(b p) f -> p b f", p=P)).then_inc(in_w, 16)

            def drain(st, dsts):
                for k, (dst, src) in enumerate(dsts):
                    act.wait_ge(full[st], k + 1)
                    act.activation(dst, src, ACT.Copy).then_inc(kept[st], 1)

            def feat_dst(buf):
                return [(buf[:, c, i * CH:(i + 1) * CH], ps[:, c * NC + i, :])
                        for c in range(FB) for i in range(NC)]

            drain("xwT", feat_dst(feat_2))
            drain("f1", [(f1[:, h, i * CH:(i + 1) * CH], ps[:, (h * NC + i) % 8, :])
                         for h in range(H) for i in range(NC)])

            def attention(ps_no, pair):
                g0 = 64 * ps_no + 32 * pair
                with act.Fori(0, NB // 2) as m:
                    def tanh(k):
                        h = 2 * pair + k % 2
                        act.wait_ge(att_free, 4 * m + (g0 + k + 1))
                        act.activation(att[:, k, :], f1[:, h, :], ACT.Tanh, scale=0.5,
                                       bias=f2_half[:, bass.ds(2 * m + k // 2, 1), h]).then_inc(tanh_done, 1)

                    def expo(k):
                        act.wait_ge(tanh_done, 4 * m + (g0 + k + 1))
                        act.activation(att[:, k, :], att[:, k, :], ACT.Exp, scale=0.5).then_inc(exp_done, 1)

                    tanh(0)
                    tanh(1)
                    expo(0)
                    tanh(2)
                    expo(1)
                    tanh(3)
                    expo(2)
                    expo(3)

            act.wait_ge(kept["f1"], H * NC)
            act.wait_ge(kept["f2"], 1)
            attention(0, 0)
            attention(0, 1)
            drain("xcT", feat_dst(feat_1))

            elu_n = 0

            def elu_parts(st, bias):
                nonlocal elu_n
                for k in range(8):
                    b = par[:, bias, k // NC:k // NC + 1] if bias is not None else 0.0
                    act.wait_ge(full[st], k + 1)
                    if elu_n >= 2:
                        act.wait_ge(elu_free, elu_n - 1)
                    e = act.activation(e_tmp[:, elu_n % 2, :], ps[:, k, :], ACT.Exp, bias=b)
                    e.then_inc(elu_e, 1)
                    act.activation(r_tmp[:, elu_n % 2, :], ps[:, k, :], ACT.Relu, bias=b).then_inc(kept[st], 1)
                    elu_n += 1

            act.wait_ge(in_w, 80)
            elu_parts("enc", BIAS_ENC)
            drain("emb", [(yh[:, 2 * k:2 * k + 2, :], ps[:, k, :].rearrange("p (b f) -> p b f", b=2)) for k in range(8)])
            attention(1, 0)
            attention(1, 1)
            drain("yT", feat_dst(feat_1))
            elu_parts("yw", None)
            elu_parts("dec", BIAS_DEC)

            def drain_ax(st):
                with act.Fori(0, NC) as m:
                    for c in range(FB):
                        act.wait_ge(full[st], FB * m + (c + 1))
                        act.activation(feat_3[:, c:c + 1, bass.ds(m * CH, CH)], ps[:, bass.ds(FB * m + c, 1), :],
                                       ACT.Copy).then_inc(kept[st], 1)

            drain_ax("ax1")
            drain("x2T", feat_dst(feat_1))

            def softmax_exp(ib, b):
                act.wait_ge(max_ready, ib + 1)
                act.activation(prob[:, b, :], ps[:, 0:4, :], ACT.Exp, bias=neg_max[:, b:b + 1],
                               accum_out=row_sum[:, bass.ds(ib, 1)]).then_inc(p_ready, 1)

            def drains(ib, b):
                for q, bank in ((0, 4), (2, 6)):
                    act.wait_ge(t_full, 4 * ib + q + 1)
                    act.activation(prob_t[:, b, q * BPC:(q + 1) * BPC, :],
                                   ps[:, bank, :].rearrange("p (k i) -> p k i", k=BPC),
                                   ACT.Copy).then_inc(t_act, 1)

            softmax_exp(0, 0)
            with act.Fori(0, NB // 2 - 1) as m:
                drains(2 * m, 0)
                softmax_exp(2 * m + 1, 1)
                drains(2 * m + 1, 1)
                softmax_exp(2 * m + 2, 0)
            drains(NB - 2, 0)
            softmax_exp(NB - 1, 1)
            drains(NB - 1, 1)

            drain_ax("ax3")

        @block.vector
        def _(v):
            steps = 0

            def step(ins):
                nonlocal steps
                steps += 1
                ins.then_inc(dve, 1)
                v.wait_ge(dve, steps)

            v.memset(xw[:, :, :, D:D + 1], 1.0).then_inc(consts, 1)
            for k in range(8):
                v.wait_ge(full["xw"], k + 1)
                v.tensor_copy(xw[:, 2 * k:2 * k + 2, :, 0:D],
                              ps[:, k, :].rearrange("p (b h d) -> p b h d", b=2, h=H)).then_inc(kept["xw"], 1)
            v.wait_ge(full["f2"], 1)
            v.tensor_scalar(f2_half[:], ps[:, 7, 0:NB * H].rearrange("p (b h) -> p b h", h=H), 0.5, None,
                            ALU.mult).then_inc(kept["f2"], 1)

            def mask(ps_no, pair):
                g0 = 64 * ps_no + 32 * pair
                with v.Fori(0, NB // 2) as m:
                    for k in range(4):
                        if ps_no == 0 and pair == 0 and k % 2 == 0:
                            v.wait_ge(adj_cast, 2 * m + k // 2 + 1)
                        v.wait_ge(exp_done, 4 * m + (g0 + k + 1))
                        v.tensor_tensor(att[:, k:k + 1, :], att[:, k:k + 1, :], adj_t[:, bass.ds(2 * m + k // 2, 1), :],
                                        ALU.mult).then_inc(mask_done, 1)

            def take_heads(ps_no, pair):
                wid = D + 1 if ps_no == 0 else D
                v.wait_ge(att_free, 4 + 64 * ps_no + 32 * pair + 32)
                groups = [(h2, b3, PER_BANK * b3, min(NB - PER_BANK * b3, PER_BANK))
                          for h2 in range(2) for b3 in range(HEAD_BANKS)]

                def acc(h2, b3, cnt):
                    return ps[:, HEAD_BANKS * h2 + b3, 0:cnt * wid].rearrange("p (b e) -> p b e", e=wid)

                if ps_no == 0:
                    for h2, b3, i0, cnt in groups:
                        ins = v.tensor_scalar(sums[:, h2, i0:i0 + cnt], acc(h2, b3, cnt)[:, :, D], TINY, None, ALU.max)
                    step(ins)
                    step(v.reciprocal(rinv[:, 2 * pair:2 * pair + 2, :], sums[:]))
                for n, (h2, b3, i0, cnt) in enumerate(groups):
                    h = 2 * pair + h2
                    ins = v.tensor_tensor(nodes[:, i0:i0 + cnt, h * D:(h + 1) * D], acc(h2, b3, cnt)[:, :, 0:D],
                                          rinv[:, h, i0:i0 + cnt].unsqueeze(2).broadcast_to([P, cnt, D]), ALU.mult)
                ins.then_inc(acc_kept, 1)

            pows = 0

            def batchnorm(buf, gain, shift, ready):
                nonlocal pows
                for c in range(FB):
                    for i in range(NC):
                        ready(c * NC + i)
                        ins = v.bn_stats(bn_st[:, c, i, :], buf[:, c, i * CH:(i + 1) * CH])
                step(ins)
                for c in range(FB):
                    ins = v.bn_aggr(bn_mv[:, c, :], bn_st[:, c, :, :])
                step(ins)
                v.tensor_scalar(bn_ve[:], bn_mv[:, :, 1], EPS_BN, None, ALU.add).then_inc(var_ready, 1)
                pows += 1
                v.wait_ge(rstd_ready, pows)
                step(v.tensor_tensor(bn_a[:], bn_rs[:], par[:, gain, :], ALU.mult))
                step(v.tensor_tensor(bn_t[:], bn_mv[:, :, 0], bn_a[:], ALU.mult))
                step(v.tensor_tensor(bn_b[:], par[:, shift, :], bn_t[:], ALU.subtract))
                for c in range(FB):
                    v.tensor_scalar(buf[:, c, :], buf[:, c, :], bn_a[:, c:c + 1], bn_b[:, c:c + 1],
                                    ALU.mult, ALU.add).then_inc(bn_done, 1)

            elu_n = 0

            def elu_join(st, dst, residual):
                nonlocal elu_n
                for k in range(8):
                    c, i = divmod(k, NC)
                    cols = dst[:, c, i * CH:(i + 1) * CH]
                    v.wait_ge(elu_e, elu_n + 1)
                    v.wait_ge(kept[st], k + 1)
                    ins = v.scalar_tensor_tensor(cols, e_tmp[:, elu_n % 2, :], 1.0, r_tmp[:, elu_n % 2, :], ALU.min, ALU.add)
                    ins.then_inc(elu_free, 1)
                    elu_n += 1
                    v.wait_ge(elu_free, elu_n)
                    if residual is not None:
                        ins = v.scalar_tensor_tensor(cols, cols, -1.0, residual[:, c, i * CH:(i + 1) * CH], ALU.add, ALU.add)
                    else:
                        ins = v.tensor_scalar(cols, cols, -1.0, None, ALU.add)
                    ins.then_inc(elu_done, 1)

            def layernorm_tail():
                nonlocal pows
                for b in range(NB):
                    ins = v.bn_aggr(ln_mv[:, b, :], ln_st[:, b, :])
                step(ins)
                v.tensor_scalar(ln_ve[:], ln_mv[:, :, 1], EPS_LN, None, ALU.add).then_inc(var_ready, 1)
                pows += 1
                v.wait_ge(rstd_ready, pows)
                for b in range(NB):
                    v.tensor_scalar(x_now[:, b, :], x_now[:, b, :], ln_mv[:, b, 0:1], ln_rs[:, b:b + 1],
                                    ALU.subtract, ALU.mult).then_inc(ln_done, 1)

            mask(0, 0)
            take_heads(0, 0)
            mask(0, 1)
            take_heads(0, 1)
            v.wait_ge(in_w, 80)
            batchnorm(feat_1, G_ENC, B_ENC, lambda k: v.wait_ge(kept["xcT"], k + 1))
            elu_join("enc", feat_2, feat_1)
            batchnorm(feat_2, G_ENC2, B_ENC2, lambda k: v.wait_ge(elu_done, k + 1))
            mask(1, 0)
            take_heads(1, 0)
            mask(1, 1)
            take_heads(1, 1)
            v.wait_ge(full["deg"], NB)
            v.tensor_copy(deg[:], ps[:, 6, 0:NB]).then_inc(kept["deg"], 1)
            elu_join("yw", feat_2, None)
            elu_join("dec", feat_1, feat_2)
            batchnorm(feat_1, G_DEC, B_DEC, lambda k: v.wait_ge(elu_done, 16 + k + 1))

            v.wait_ge(kept["deg"], 1)
            v.tensor_scalar(deg1[:], deg[:], 1.0, None, ALU.add).then_inc(var_ready, 1)
            v.tensor_scalar(deg3[:], deg[:], EPS_DEG, None, ALU.add).then_inc(var_ready, 1)
            pows += 2

            for k in range(8):
                v.wait_ge(full["l0"], k + 1)
                for b in (2 * k, 2 * k + 1):
                    o = (b % 2) * F
                    ins = v.tensor_tensor(x_now[:, b, :], ps[:, k, o:o + F], x_now[:, b, :], ALU.add)
                ins.then_inc(kept["l0"], 1)
                v.wait_ge(kept["l0"], k + 1)
                for b in (2 * k, 2 * k + 1):
                    ins = v.bn_stats(ln_st[:, b, :], x_now[:, b, :])
            step(ins)
            layernorm_tail()

            cuts = 0

            def cut(dinv, norms):
                nonlocal cuts
                v.wait_ge(ln_done, NB * norms)
                step(v.tensor_tensor(nodes, x_now[:], dinv.unsqueeze(2).broadcast_to([P, NB, F]), ALU.mult))
                for s in range(3):
                    ins = v.tensor_copy(parts[:, s], nodes)
                    ins.then_inc(part_ready, 1)
                    if s < 2:
                        v.wait_ge(part_ready, 3 * cuts + s + 1)
                        step(v.tensor_tensor(nodes, nodes, parts[:, s], ALU.subtract))
                cuts += 1

            cut(dinv1[:], 1)

            def gcn_tail(st, dinv, last):
                for k in range(8):
                    v.wait_ge(full[st], k + 1)
                    for b in (2 * k, 2 * k + 1):
                        z = ps[:, k, (b % 2) * F:(b % 2) * F + F]
                        if last:
                            ins = v.scalar_tensor_tensor(nodes[:, b, :], z, dinv[:, b:b + 1], row_s[:, 1, :], ALU.mult, ALU.add)
                        else:
                            ins = v.tensor_scalar(nodes[:, b, :], z, dinv[:, b:b + 1], 0.0, ALU.mult, ALU.max)
                    ins.then_inc(kept[st], 1)
                    v.wait_ge(kept[st], k + 1)
                    for b in (2 * k, 2 * k + 1):
                        ins = v.tensor_tensor(x_now[:, b, :], x_now[:, b, :], nodes[:, b, :], ALU.add)
                    step(ins)
                    for b in (2 * k, 2 * k + 1):
                        ins = v.bn_stats(ln_st[:, b, :], x_now[:, b, :])
                step(ins)

            gcn_tail("z1", dinv1, False)
            layernorm_tail()

            for k in range(16):
                c, i = divmod(k % 8, NC)
                dst = (feat_2 if k < 8 else feat_3)[:, c, i * CH:(i + 1) * CH]
                v.wait_ge(full["qk"], k + 1)
                if k < 8:
                    ins = v.tensor_scalar(dst, ps[:, k % 8, :], par[:, BIAS_Q, c:c + 1], 1.0 / 16, ALU.add, ALU.mult)
                else:
                    ins = v.tensor_scalar(dst, ps[:, k % 8, :], par[:, BIAS_K, c:c + 1], None, ALU.add)
                ins.then_inc(kept["qk"], 1)
            for k in range(8):
                v.wait_ge(full["v"], k + 1)
                v.tensor_tensor(nodes[:, 2 * k:2 * k + 2, :], ps[:, k, :].rearrange("p (b f) -> p b f", b=2),
                                row_s[:, 0:1, :].broadcast_to([P, 2, F]), ALU.add).then_inc(kept["v"], 1)

            def row_max(ib, b):
                v.wait_ge(s_full, ib + 1)
                v.tensor_reduce(neg_max[:, b:b + 1], ps[:, 0:4, :], AX.XY, ALU.max, negate=True).then_inc(max_ready, 1)

            def tail(ib, b):
                for q, bank in ((1, 5), (3, 4)):
                    v.wait_ge(t_full, 4 * ib + q + 1)
                    v.tensor_copy(prob_t[:, b, q * BPC:(q + 1) * BPC, :],
                                  ps[:, bank, :].rearrange("p (k i) -> p k i", k=BPC)).then_inc(t_dve, 1)

            def finish(ib, b):
                v.wait_ge(p_ready, ib + 1)
                v.reciprocal(row_inv[:, bass.ds(ib, 1)], row_sum[:, bass.ds(ib, 1)]).then_inc(mean_inv, 1)
                v.wait_ge(o_full, ib + 1)
                v.wait_ge(mean_inv, ib + 1)
                v.scalar_tensor_tensor(x_now[:, bass.ds(ib, 1), :], ps[:, 7:8, 0:F], row_inv[:, bass.ds(ib, 1)],
                                       x_now[:, bass.ds(ib, 1), :], ALU.mult, ALU.add).then_inc(o_kept, 1)
                v.wait_ge(o_kept, ib + 1)
                return v.bn_stats(ln_st[:, bass.ds(ib, 1), :], x_now[:, bass.ds(ib, 1), :])

            row_max(0, 0)
            with v.Fori(0, NB // 2 - 1) as m:
                tail(2 * m, 0)
                row_max(2 * m + 1, 1)
                finish(2 * m, 0)
                tail(2 * m + 1, 1)
                row_max(2 * m + 2, 0)
                finish(2 * m + 1, 1)
            tail(NB - 2, 0)
            row_max(NB - 1, 1)
            finish(NB - 2, 0)
            tail(NB - 1, 1)
            step(finish(NB - 1, 1))
            layernorm_tail()
            cut(dinv3[:], 3)
            gcn_tail("z3", dinv3, True)
            layernorm_tail()

        @block.tensor
        def _(pe):
            def feature_product(st, w, src, first=lambda k: None, ready=lambda k: None):
                for e in range(FB):
                    for i in range(NC):
                        k = e * NC + i
                        first(k)
                        ready(i)
                        for f in range(FB):
                            mm = pe.matmul(ps[:, k, :], w_all[:, w, f, e * P:(e + 1) * P],
                                           src[:, f, i * CH:(i + 1) * CH], start=f == 0, stop=f == FB - 1)
                        mm.then_inc(full[st], 1)

            def node_product(st, w, src, first=lambda k: None):
                for k in range(8):
                    first(k)
                    for b in (2 * k, 2 * k + 1):
                        o = (b % 2) * F
                        for f in range(FB):
                            mm = pe.matmul(ps[:, k, o:o + F], src[:, f, b * P:(b + 1) * P],
                                           w_all[:, w, f, :], start=f == 0, stop=f == FB - 1)
                    mm.then_inc(full[st], 1)

            def to_features(st, src, first=lambda k: None):
                for c in range(FB):
                    for i in range(NC):
                        first(c * NC + i)
                        for t in range(BPC):
                            mm = pe.transpose(ps[:, c * NC + i, t * P:(t + 1) * P],
                                              src[:, i * BPC + t, c * P:(c + 1) * P], ident[:])
                        mm.then_inc(full[st], 1)

            def to_nodes(st, src, first=lambda k: None):
                for k in range(8):
                    first(k)
                    for b in (2 * k, 2 * k + 1):
                        for c in range(FB):
                            mm = pe.transpose(ps[:, k, (b % 2) * F + c * P:(b % 2) * F + (c + 1) * P],
                                              src[:, c, b * P:(b + 1) * P], ident[:])
                    mm.then_inc(full[st], 1)
                return mm

            pe.wait_ge(in_x, 64)
            pe.wait_ge(consts, 5)
            for c in range(FB):
                for i in range(NC):
                    pe.matmul(ps[:, c * NC + i, :], wbd_s[:, c, :], feat_1[:, c, i * CH:(i + 1) * CH],
                              start=True, stop=True).then_inc(full["xwT"], 1)
            for k in range(8):
                pe.wait_ge(kept["xwT"], k + 1)
                for b in (2 * k, 2 * k + 1):
                    for c in range(FB):
                        o = (b % 2) * F + c * P
                        mm = pe.matmul(ps[:, k, o:o + P], feat_1[:, c, b * P:(b + 1) * P], wbd_s[:, c, :],
                                       start=True, stop=True)
                mm.then_inc(full["xw"], 1)
            pe.wait_ge(kept["xw"], 8)
            for c in range(FB):
                for b in range(NB):
                    mm = pe.matmul(ps[:, 7, b * H + 2 * c:b * H + 2 * c + 2], feat_2[:, c, b * P:(b + 1) * P],
                                   v1_s[:, c, :], start=True, stop=True)
            mm.then_inc(full["f2"], 1)
            for h in range(H):
                for i in range(NC):
                    k = h * NC + i
                    if k == 7:
                        pe.wait_ge(kept["f2"], 1)
                    if k >= 8:
                        pe.wait_ge(kept["f1"], k - 7)
                    mm = pe.matmul(ps[:, k % 8, :], v0_s[:, h, :], feat_2[:, h // 2, i * CH:(i + 1) * CH],
                                   start=True, stop=True)
                    mm.then_inc(full["f1"], 1)

            def degrees():
                pe.wait_ge(adj_cast, NB)
                with pe.Fori(0, NB) as b:
                    for j in range(NB):
                        mm = pe.matmul(ps[:, 6, bass.ds(b, 1)], adj_t[:, j, bass.ds(b * P, P)], ones_b[:],
                                       start=j == 0, stop=j == NB - 1)
                    mm.then_inc(full["deg"], 1)

            def attend(ps_no, pair, mov):
                wid = D + 1 if ps_no == 0 else D
                n = 2 * ps_no + pair
                g0 = 64 * ps_no + 32 * pair
                if n:
                    pe.wait_ge(acc_kept, n)
                for b in range(2 * HEAD_BANKS):
                    pe.matmul(ps[:, b, :], zeros_b[:, 0:P], zeros_b[:], start=True, stop=True, skip_group_check=True)
                with pe.Fori(0, NB // 2) as m:
                    for k in range(4):
                        pe.wait_ge(mask_done, 4 * m + (g0 + k + 1))
                        for b in range(NB):
                            o = (b % PER_BANK) * wid
                            mm = pe.matmul(ps[:, HEAD_BANKS * (k % 2) + b // PER_BANK, o:o + wid],
                                           att[:, k, b * P:(b + 1) * P],
                                           mov[:, bass.ds(2 * m + k // 2, 1), 2 * pair + k % 2, :],
                                           start=False, stop=True, skip_group_check=True)
                        mm.then_inc(att_free, 1)

            pe.wait_ge(kept["f1"], H * NC)
            attend(0, 0, xw)
            attend(0, 1, xw)
            pe.wait_ge(acc_kept, 2)
            to_features("xcT", nodes)
            pe.wait_ge(in_w, 80)
            pe.wait_ge(kept["xcT"], 8)
            pe.wait_ge(bn_done, 2)
            feature_product("enc", W_ENC, feat_1)
            pe.wait_ge(bn_done, 4)
            to_nodes("emb", feat_2, first=lambda k: pe.wait_ge(kept["enc"], k + 1))
            pe.wait_ge(kept["emb"], 8)
            yh4 = yh.rearrange("p b (h d) -> p b h d", h=H)
            attend(1, 0, yh4)
            degrees()
            attend(1, 1, yh4)
            pe.wait_ge(acc_kept, 4)
            pe.wait_ge(kept["deg"], 1)
            to_features("yT", nodes)
            pe.wait_ge(kept["yT"], 8)
            for c in range(FB):
                for i in range(NC):
                    pe.matmul(ps[:, c * NC + i, :], wtbd_s[:, c, :], feat_1[:, c, i * CH:(i + 1) * CH],
                              start=True, stop=True).then_inc(full["yw"], 1)
            pe.wait_ge(elu_done, 16)
            feature_product("dec", W_DEC, feat_2, first=lambda k: pe.wait_ge(kept["yw"], k + 1))
            pe.wait_ge(bn_done, 6)
            to_nodes("l0", feat_1, first=lambda k: pe.wait_ge(kept["dec"], k + 1))

            def neighbours(st, cuts, self_loops):
                pe.wait_ge(part_ready, 3 * cuts + 1)
                with pe.Fori(0, NC) as m:
                    for c in range(FB):
                        bank = ps[:, bass.ds(FB * m + c, 1), :]
                        for s in range(3):
                            pe.wait_ge(part_ready, 3 * cuts + s + 1)
                            for j in range(NB):
                                mm = pe.matmul(bank, parts[:, s, j, c * P:(c + 1) * P],
                                               adj_t[:, j, bass.ds(m * CH, CH)], start=s == 0 and j == 0,
                                               stop=s == 2 and j == NB - 1, skip_group_check=True)
                            if self_loops:
                                for t in range(BPC):
                                    mm = pe.matmul(ps[:, bass.ds(FB * m + c, 1), t * P:(t + 1) * P],
                                                   parts[:, s, bass.ds(m * BPC + t, 1), c * P:(c + 1) * P], eye_b[:],
                                                   start=False, stop=s == 2, skip_group_check=True)
                        mm.then_inc(full[st], 1)

            pe.wait_ge(kept["l0"], 8)
            neighbours("ax1", 0, True)
            pe.wait_ge(kept["ax1"], 8)
            node_product("z1", W_L1, feat_3)

            pe.wait_ge(ln_done, 2 * NB)
            to_features("x2T", x_now, first=lambda k: pe.wait_ge(kept["z1"], k + 1))
            pe.wait_ge(kept["x2T"], 8)
            feature_product("qk", W_Q, feat_1)
            feature_product("qk", W_K, feat_1, first=lambda k: pe.wait_ge(kept["qk"], k + 1))
            node_product("v", W_V, feat_1, first=lambda k: pe.wait_ge(kept["qk"], 8 + k + 1))
            pe.wait_ge(kept["v"], 8)

            def scores(ib, b, free):
                pe.wait_ge(q_ready, ib + 1)
                if free:
                    pe.wait_ge(p_ready, ib)
                for jc in range(NC):
                    for f in range(FB):
                        pe.matmul(ps[:, jc, :], q_blk[:, b, f, :], feat_3[:, f, jc * CH:(jc + 1) * CH],
                                  start=f == 0, stop=False, skip_group_check=True)
                    for t in range(BPC):
                        mm = pe.matmul(ps[:, jc, t * P:(t + 1) * P], adj_t[:, jc * BPC + t, bass.ds(ib * P, P)],
                                       two_b[:], start=False, stop=True, skip_group_check=True)
                mm.then_inc(s_full, 1)

            def values(ib, b, first=False):
                pe.wait_ge(p_ready, ib + 1)
                for q, bank in enumerate((4, 5, 6, 4)):
                    if q == 3:
                        pe.wait_ge(t_act, 2 * ib + 1)
                    elif not first:
                        if q == 1:
                            pe.wait_ge(t_dve, 2 * ib - 1)
                        elif q == 0:
                            pe.wait_ge(t_dve, 2 * ib)
                        else:
                            pe.wait_ge(t_act, 2 * ib)
                    for t in range(BPC):
                        j = q * BPC + t
                        mm = pe.transpose(ps[:, bank, t * P:(t + 1) * P], prob[:, b, j * P:(j + 1) * P], ident[:])
                    mm.then_inc(t_full, 1)
                if not first:
                    pe.wait_ge(o_kept, ib)
                for q in range(NC):
                    pe.wait_ge(t_act if q % 2 == 0 else t_dve, 2 * ib + q // 2 + 1)
                    for t in range(BPC):
                        j = q * BPC + t
                        mm = pe.matmul(ps[:, 7, 0:F], prob_t[:, b, j, :], nodes[:, j, :],
                                       start=j == 0, stop=j == NB - 1)
                mm.then_inc(o_full, 1)

            scores(0, 0, False)
            scores(1, 1, True)
            values(0, 0, first=True)
            with pe.Fori(0, NB // 2 - 1) as m:
                scores(2 * m + 2, 0, True)
                values(2 * m + 1, 1)
                scores(2 * m + 3, 1, True)
                values(2 * m + 2, 0)
            values(NB - 1, 1)

            pe.wait_ge(ln_done, 3 * NB)
            neighbours("ax3", 1, False)
            pe.wait_ge(kept["ax3"], 8)
            node_product("z3", W_L3, feat_3)


def kernel(x, adj, L0_gnn_W, L0_gnn_V, L0_gnn_enc_bn_gamma, L0_gnn_enc_bn_beta, L0_gnn_enc_mlp_W,
           L0_gnn_enc_mlp_b, L0_gnn_enc_mlp_bn_gamma, L0_gnn_enc_mlp_bn_beta, L0_gnn_dec_mlp_W,
           L0_gnn_dec_mlp_b, L0_gnn_dec_mlp_bn_gamma, L0_gnn_dec_mlp_bn_beta, L1_gnn_W,
           L2_gnn_Wq, L2_gnn_bq, L2_gnn_Wk, L2_gnn_bk, L2_gnn_Wv, L2_gnn_bv, L3_gnn_W, L3_gnn_b):
    import numpy as np
    import concourse.bacc as bacc
    from concourse.bass_utils import run_bass_kernel_spmd

    W, V = np.asarray(L0_gnn_W), np.asarray(L0_gnn_V)
    wbd = np.zeros((FB, P, P), W.dtype)
    wtbd = np.zeros((FB, P, P), W.dtype)
    v0rep = np.zeros((H, P, P), V.dtype)
    v1 = np.zeros((FB, P, 2), V.dtype)
    for h in range(H):
        c, r = divmod(h, 2)
        rows = slice(r * D, (r + 1) * D)
        wbd[c, rows, rows] = W[h]
        wtbd[c, rows, rows] = W[h].T
        v0rep[h, rows, :] = V[h, 0]
        v1[c, rows, r] = V[h, 1, :, 0]

    def blocks(w):
        return np.asarray(w).reshape(FB, P, F).transpose(1, 0, 2)

    weights = np.stack([blocks(np.asarray(L0_gnn_enc_mlp_W).T), blocks(np.asarray(L0_gnn_dec_mlp_W).T),
                        blocks(L1_gnn_W), blocks(L2_gnn_Wq), blocks(L2_gnn_Wk), blocks(L2_gnn_Wv),
                        blocks(np.asarray(L3_gnn_W).T)], axis=1)
    params = np.stack([np.asarray(a).reshape(FB, P).T for a in (
        L0_gnn_enc_bn_gamma, L0_gnn_enc_bn_beta, L0_gnn_enc_mlp_b, L0_gnn_enc_mlp_bn_gamma,
        L0_gnn_enc_mlp_bn_beta, L0_gnn_dec_mlp_b, L0_gnn_dec_mlp_bn_gamma, L0_gnn_dec_mlp_bn_beta,
        L2_gnn_bq, L2_gnn_bk)], axis=1)
    rows = np.stack([np.broadcast_to(np.asarray(a), (P, F)) for a in (L2_gnn_bv, L3_gnn_b)], axis=1)
    x, adj = np.asarray(x), np.asarray(adj)
    arrays = {k: np.ascontiguousarray(a) for k, a in dict(
        x=x, xT=x.T, adjT=adj.T, wbd=wbd, wtbd=wtbd, v0rep=v0rep, v1=v1, weights=weights,
        params=params, rows=rows).items()}

    nc = bacc.Bacc("TRN2", target_bir_lowering=False, num_devices=1)
    aps = {k: nc.dram_tensor("in_" + k, a.shape, mybir.dt.from_np(a.dtype), kind="ExternalInput").ap()
           for k, a in arrays.items()}
    out = nc.dram_tensor("out", (N, F), F32, kind="ExternalOutput").ap()
    gnn_stack(nc, out=out, **aps)
    r = run_bass_kernel_spmd(nc, [{"in_" + k: a for k, a in arrays.items()}], core_ids=[0])
    return r.results[0]["out"]
```

```python
from contextlib import ExitStack

import concourse.bass as bass
from concourse import mybir

ACT = mybir.ActivationFunctionType
ALU = mybir.AluOpType
AX = mybir.AxisListType
F32 = mybir.dt.float32
BF16 = mybir.dt.bfloat16

P = 128
N = 2048
F = 256
H = 4
D = F // H
NB = N // P
FB = F // P
CH = 512
NC = N // CH
BPC = CH // P
EPS_BN = 1e-6
EPS_LN = 1e-5
EPS_DEG = 1e-8
MOVING = 96
GB = BPC
NG = NB // GB
TINY = 1e-30
PER_BANK = 6
HEAD_BANKS = 3

W_ENC, W_DEC, W_L1, W_Q, W_K, W_V, W_L3 = range(7)
G_ENC, B_ENC, BIAS_ENC, G_ENC2, B_ENC2, BIAS_DEC, G_DEC, B_DEC, BIAS_Q, BIAS_K = range(10)


def gnn_stack(nc, x, xT, adjT, wbd, wtbd, v0rep, v1, weights, params, rows, out):
    with ExitStack() as ctx:
        def sb(name, shape, dt=F32):
            return ctx.enter_context(nc.sbuf_tensor(name, shape, dt))

        def sem(name):
            return ctx.enter_context(nc.semaphore(name))

        adj_t = sb("adj_t", [P, NB, N], BF16)
        f1_all = sb("f1_all", [P, H * N])
        big = sb("big", [P, 4 * N])
        node_b = sb("node_b", [P, NB * F])
        node_a = sb("node_a", [P, NB * F])
        x_now = sb("x_now", [P, NB, F])
        w_all = sb("w_all", [P, 7, FB, F])
        wtbd_s = sb("wtbd_s", [P, FB, P])
        v0_s = sb("v0_s", [P, H, P])
        v1_s = sb("v1_s", [P, FB, 2])
        par = sb("par", [P, 10, FB])
        row_s = sb("row_s", [P, 2, F])
        ident = sb("ident", [P, P])
        credit = sb("credit", [P, 3])
        pause = sb("pause", [P, 1])
        eye_b = sb("eye_b", [P, P], BF16)
        two_b = sb("two_b", [P, P], BF16)
        zeros_b = sb("zeros_b", [P, CH], BF16)
        ones_b = sb("ones_b", [P, 1], BF16)
        minus_half = sb("minus_half", [P, GB])
        wv0_s = sb("wv0_s", [P, H, P])
        wbd_x = sb("wbd_x", [P, FB, P + 2])
        mov_s = sb("mov_s", [P, 4, MOVING])
        f2_half = sb("f2_half", [P, NB, H])
        deg = sb("deg", [P, NB])
        dinv = sb("dinv", [P, 2, NG, GB])
        sums = sb("sums", [P, 2, NB])
        rinv = sb("rinv", [P, H, NB])
        bn_st = sb("bn_st", [P, FB, NC, 6])
        bn_mv = sb("bn_mv", [P, FB, 2])
        bn_ve = sb("bn_ve", [P, FB])
        bn_rs = sb("bn_rs", [P, FB])
        bn_a = sb("bn_a", [P, FB])
        bn_t = sb("bn_t", [P, FB])
        bn_b = sb("bn_b", [P, FB])
        ln_st = sb("ln_st", [P, 2, GB, 6])
        ln_mv = sb("ln_mv", [P, 2, GB, 2])
        ln_ve = sb("ln_ve", [P, 2, GB])
        ln_rs = sb("ln_rs", [P, 2, GB])
        deg_ve = sb("deg_ve", [P, 2, NG, GB])
        q_blk = sb("q_blk", [P, 2, FB, P])
        neg_max = sb("neg_max", [P, 2])
        row_sum = sb("row_sum", [P, NB])
        row_inv = sb("row_inv", [P, NB])

        feat_1 = big[:, 0:2 * N].rearrange("p (c n) -> p c n", c=FB)
        feat_2 = big[:, 2 * N:4 * N].rearrange("p (c n) -> p c n", c=FB)
        att = big[:, :].rearrange("p (k n) -> p k n", k=4)
        x_t = x_now[:, :, :].rearrange("p b f -> p (b f)").rearrange("p (c n) -> p c n", c=FB)
        yh = node_b[:, :].rearrange("p (b f) -> p b f", b=NB)
        feat_3 = node_b[:, :].rearrange("p (c n) -> p c n", c=FB)
        e_tmp = node_b[:, 0:2 * CH].rearrange("p (k n) -> p k n", k=2)
        r_tmp = node_b[:, 2 * CH:4 * CH].rearrange("p (k n) -> p k n", k=2)
        ax_chunk = node_b[:, 0:FB * CH].rearrange("p (c n) -> p c n", c=FB)
        nodes = node_a[:, :].rearrange("p (b f) -> p b f", b=NB)
        adj_row = node_a[:, :].rearrange("p (k n) -> p k n", k=2)
        f1 = f1_all[:, :].rearrange("p (h n) -> p h n", h=H)
        prob = f1_all[:, 0:2 * N].rearrange("p (k n) -> p k n", k=2)
        prob_t = f1_all[:, 2 * N:4 * N].rearrange("p (k b i) -> p k b i", k=2, b=NB)
        w_flat = w_all[:, :, :, :].rearrange("p w c f -> p (w c f)")

        def bf16_nodes(words):
            return words.bitcast(BF16).rearrange("p (b f) -> p b f", b=NB)

        half = NB * F // 2
        parts = [[bf16_nodes(big[:, s * half:(s + 1) * half]) for s in range(3)],
                 [bf16_nodes(big[:, 0:half]), bf16_nodes(big[:, half:2 * half]), bf16_nodes(w_flat[:, 0:half])]]
        rest = [nodes, w_flat[:, half:half + GB * F].rearrange("p (b f) -> p b f", b=GB)]

        ps = ctx.enter_context(nc.psum_tensor("ps", [P, 8, CH], F32))

        in_x = sem("in_x")
        in_h = sem("in_h")
        in_w = sem("in_w")
        adj_in = [sem("adj_in0"), sem("adj_in1")]
        adj_cast = sem("adj_cast")
        consts = sem("consts")
        const_a = sem("const_a")
        full = {}
        kept = {}
        for st in ("wv", "f1", "xw", "deg", "xcT", "enc", "emb", "yT", "yw", "dec", "l0",
                   "ax", "z", "x2T", "qk", "v"):
            full[st] = sem("full_" + st)
            kept[st] = sem("kept_" + st)
        f1_late = sem("f1_late")
        f2_kept = sem("f2_kept")
        elu_e = sem("elu_e")
        elu_free = sem("elu_free")
        elu_done = sem("elu_done")
        dve = sem("dve")
        tanh_done = sem("tanh_done")
        exp_done = sem("exp_done")
        mask_done = sem("mask_done")
        mov_ready = sem("mov_ready")
        att_free = sem("att_free")
        acc_kept = sem("acc_kept")
        var_ready = sem("var_ready")
        rstd_ready = sem("rstd_ready")
        bn_done = sem("bn_done")
        ln_stats = sem("ln_stats")
        ln_aggr = sem("ln_aggr")
        ln_var = sem("ln_var")
        ln_rstd = sem("ln_rstd")
        ln_done = sem("ln_done")
        z_scaled = sem("z_scaled")
        z_added = sem("z_added")
        cut_rest = [sem(f"cut_rest{s}") for s in range(3)]
        part_ready = [sem(f"part_ready{s}") for s in range(3)]
        q_ready = sem("q_ready")
        s_full = sem("s_full")
        max_ready = sem("max_ready")
        p_ready = sem("p_ready")
        t_full = sem("t_full")
        t_act = sem("t_act")
        t_dve = sem("t_dve")
        o_full = sem("o_full")
        o_kept = sem("o_kept")
        inv_ready = sem("inv_ready")
        out_done = sem("out_done")

        PAIR = 2 * NB
        PASS = 2 * PAIR
        block = ctx.enter_context(nc.Block())

        @block.sync
        def _(sp):
            sp.dma_start(wtbd_s[:], wtbd.rearrange("c p e -> p c e")).then_inc(in_h, 16)
            sp.dma_start(v0_s[:], v0rep.rearrange("h p e -> p h e")).then_inc(in_h, 16)
            for c in range(FB):
                sp.dma_start(x_t[:, c, :], xT[c * P:(c + 1) * P, :]).then_inc(in_x, 16)
            for s in range(2):
                sp.dma_start(adj_row[:, s, :], adjT[s * P:(s + 1) * P, :]).then_inc(adj_in[s], 16)
            with sp.Fori(1, NB // 2) as m:
                for s in range(2):
                    sp.wait_ge(adj_cast, 2 * m + s - 1)
                    sp.dma_start(adj_row[:, s, :], adjT[bass.ds((2 * m + s) * P, P), :]).then_inc(adj_in[s], 16)
            out_v = out.rearrange("(b p) f -> p b f", p=P)
            with sp.Fori(0, NG) as g:
                sp.wait_ge(ln_done, g + (3 * NG + 1))
                sp.dma_start(out_v[:, bass.ds(g * GB, GB), :], x_now[:, bass.ds(g * GB, GB), :]).then_inc(out_done, 16)
            sp.wait_ge(out_done, 16 * NG)

        @block.gpsimd
        def _(pool):
            pool.memset(ident[:], 0.0).then_inc(const_a, 1)
            pool.memset(eye_b[:], 0.0).then_inc(const_a, 1)
            pool.memset(two_b[:], 0.0).then_inc(const_a, 1)
            pool.memset(zeros_b[:], 0.0).then_inc(consts, 1)
            pool.memset(ones_b[:], 1.0).then_inc(att_free, 4)
            pool.memset(mov_s[:, :, D:D + 1], 1.0).then_inc(consts, 1)
            pool.memset(mov_s[:, :, D + 1:MOVING], 0.0).then_inc(consts, 1)
            for n, (s_, c) in enumerate(((kept["ax"], 2), (kept["z"], 2), (full["z"], 2))):
                pool.memset(credit[:, n:n + 1], 0.0).then_inc(s_, c)
            pool.memset(minus_half[:], -0.5).then_inc(const_a, 1)
            pool.wait_ge(const_a, 4)
            for m, v in ((ident, 1.0), (eye_b, 1.0), (two_b, 2.0)):
                pool.affine_select(out=m[:], in_=m[:], compare_op=ALU.not_equal, fill=v, base=0,
                                   pattern=[[-1, P]], channel_multiplier=1).then_inc(consts, 1)

            def moving(ps_no, pair):
                g0 = PASS * ps_no + PAIR * pair
                with pool.Fori(0, NB // 2) as m:
                    for k in range(4):
                        h = 2 * pair + k % 2
                        pool.wait_ge(att_free, 4 * m + (g0 + k + 1))
                        pool.tensor_copy(mov_s[:, k:k + 1, 0:D], yh[:, bass.ds(2 * m + k // 2, 1), h * D:(h + 1) * D])\
                            .then_inc(mov_ready, 1)

            n = 0

            def power(dst, src, width):
                nonlocal n
                n += 1
                pool.wait_ge(var_ready, n)
                pool.tensor_tensor(dst, src, minus_half[:, 0:width], ALU.pow).then_inc(rstd_ready, 1)

            def ln_power(ln, g, slot):
                pool.wait_ge(ln_var, g + (NG * ln + 1))
                pool.tensor_tensor(ln_rs[:, slot, :], ln_ve[:, slot, :], minus_half[:], ALU.pow).then_inc(ln_rstd, 1)

            pool.wait_ge(kept["xw"], NB)
            moving(0, 0)
            moving(0, 1)
            power(bn_rs[:], bn_ve[:], FB)
            power(bn_rs[:], bn_ve[:], FB)
            pool.wait_ge(kept["emb"], 8)
            moving(1, 0)
            moving(1, 1)
            for l in range(2):
                for g in range(NG):
                    power(dinv[:, l, g, :], deg_ve[:, l, g, :], GB)
            power(bn_rs[:], bn_ve[:], FB)
            for g in range(NG):
                ln_power(0, g, g % 2)
            with pool.Fori(0, NG) as g:
                ln_power(1, g, 0)

            pool.wait_ge(kept["qk"], 8)
            for b in range(2):
                pool.tensor_copy(q_blk[:, b], feat_2[:, :, b * P:(b + 1) * P]).then_inc(q_ready, 1)

            def q_copies(g):
                for t in range(GB):
                    if isinstance(g, int) and g * GB + t + 2 >= NB:
                        continue
                    pool.wait_ge(s_full, GB * g + (t + 1))
                    pool.tensor_copy(q_blk[:, t % 2], feat_2[:, :, bass.ds((GB * g + (t + 2)) * P, P)]).then_inc(q_ready, 1)

            with pool.Fori(0, NG - 1) as g:
                q_copies(g)
                ln_power(2, g, 0)
            q_copies(NG - 1)
            ln_power(2, NG - 1, 0)
            with pool.Fori(0, NG) as g:
                ln_power(3, g, 0)

        @block.scalar
        def _(act):
            act.dma_start(v1_s[:], v1.rearrange("c p e -> p c e")).then_inc(in_h, 16)
            act.dma_start(wbd_x[:, :, 0:P], wbd.rearrange("c p e -> p c e")).then_inc(in_h, 16)

            def drain(st, dsts):
                for k, (dst, src) in enumerate(dsts):
                    act.wait_ge(full[st], k + 1)
                    act.activation(dst, src, ACT.Copy).then_inc(kept[st], 1)

            def feat_dst(buf):
                return [(buf[:, c, i * CH:(i + 1) * CH], ps[:, i * FB + c, :])
                        for i in range(NC) for c in range(FB)]

            drain("f1", [(f1[:, h, i * CH:(i + 1) * CH], ps[:, i, :]) for h in range(2) for i in range(NC)])

            def attention(ps_no, pair):
                g0 = PASS * ps_no + PAIR * pair
                with act.Fori(0, NB // 2) as m:
                    def tanh(k):
                        h = 2 * pair + k % 2
                        act.wait_ge(att_free, 4 * m + (g0 + k + 1))
                        act.activation(att[:, k:k + 1, :], f1[:, h:h + 1, :], ACT.Tanh, scale=0.5,
                                       bias=f2_half[:, bass.ds(2 * m + k // 2, 1), h]).then_inc(tanh_done, 1)

                    def expo(k):
                        act.wait_ge(tanh_done, 4 * m + (g0 + k + 1))
                        act.activation(att[:, k, :], att[:, k, :], ACT.Exp, scale=0.5).then_inc(exp_done, 1)

                    tanh(0)
                    for k in range(1, 4):
                        tanh(k)
                        expo(k - 1)
                    expo(3)

            act.wait_ge(f2_kept, NB)
            act.wait_ge(kept["f1"], 2 * NC)
            attention(0, 0)
            act.wait_ge(full["f1"], H * NC)
            act.wait_ge(full["xw"], NB)
            act.dma_start(par[:], params).then_inc(in_w, 16)
            act.dma_start(w_all[:], weights).then_inc(in_w, 16)
            act.dma_start(row_s[:], rows).then_inc(in_w, 16)
            act.dma_start(x_now[:], x.rearrange("(b p) f -> p b f", p=P)).then_inc(in_w, 16)
            act.wait_ge(f1_late, 2 * NC)
            attention(0, 1)
            drain("xcT", feat_dst(feat_1))

            elu_n = 0

            def elu_parts(st, bias):
                nonlocal elu_n
                for k in range(8):
                    b = par[:, bias, k % FB:k % FB + 1] if bias is not None else 0.0
                    act.wait_ge(full[st], k + 1)
                    if elu_n >= 2:
                        act.wait_ge(elu_free, elu_n - 1)
                    act.activation(e_tmp[:, elu_n % 2, :], ps[:, k, :], ACT.Exp, bias=b).then_inc(elu_e, 1)
                    act.activation(r_tmp[:, elu_n % 2, :], ps[:, k, :], ACT.Relu, bias=b).then_inc(kept[st], 1)
                    elu_n += 1

            act.wait_ge(in_w, 64)
            elu_parts("enc", BIAS_ENC)
            drain("emb", [(yh[:, 2 * k:2 * k + 2, :], ps[:, k, :].rearrange("p (b f) -> p b f", b=2)) for k in range(8)])
            attention(1, 0)
            attention(1, 1)
            drain("yT", feat_dst(feat_1))
            elu_parts("yw", None)
            elu_parts("dec", BIAS_DEC)

            for t in range(NG + 2):
                for s in range(3):
                    g = t - s
                    if 0 <= g < NG:
                        rows_g = slice(g * GB, (g + 1) * GB)
                        act.wait_ge(cut_rest[s], g + 1)
                        act.activation(parts[0][s][:, rows_g, :], rest[0][:, rows_g, :], ACT.Copy).then_inc(part_ready[s], 1)

            def drain_ax(layer):
                with act.Fori(0, NC) as m:
                    for c in range(FB):
                        act.wait_ge(full["ax"], FB * m + (8 * layer + c + 1))
                        if c == 0:
                            act.wait_ge(full["z"], 2 * m + (8 * layer + 2))
                        act.activation(ax_chunk[:, c, :], ps[:, c, :], ACT.Copy).then_inc(kept["ax"], 1)

            drain_ax(0)
            drain("x2T", feat_dst(feat_1))

            def softmax_exp(ib, b):
                act.wait_ge(max_ready, ib + 1)
                act.activation(prob[:, b, :], ps[:, 0:4, :], ACT.Exp, bias=neg_max[:, b:b + 1],
                               accum_out=row_sum[:, bass.ds(ib, 1)]).then_inc(p_ready, 1)

            def drains(ib, b):
                for q, bank in ((0, 4), (2, 6)):
                    act.wait_ge(t_full, 4 * ib + (q + 1))
                    act.activation(prob_t[:, b, q * BPC:(q + 1) * BPC, :],
                                   ps[:, bank, :].rearrange("p (k i) -> p k i", k=BPC),
                                   ACT.Copy).then_inc(t_act, 1)

            softmax_exp(0, 0)
            with act.Fori(0, NB // 2 - 1) as m:
                drains(2 * m, 0)
                softmax_exp(2 * m + 1, 1)
                drains(2 * m + 1, 1)
                softmax_exp(2 * m + 2, 0)
            drains(NB - 2, 0)
            softmax_exp(NB - 1, 1)
            drains(NB - 1, 1)

            drain_ax(1)

        @block.vector
        def _(v):
            steps = 0

            def step(ins):
                nonlocal steps
                steps += 1
                ins.then_inc(dve, 1)
                v.wait_ge(dve, steps)

            def wait_apart(sem_, count):
                v.wait_ge(sem_, count)
                v.memset(pause[:], 0.0)

            v.wait_ge(full["wv"], 1)
            v.wait_ge(in_h, 64)
            v.tensor_copy(wv0_s[:], ps[:, 7, :].rearrange("p (h e) -> p h e", h=H)).then_inc(kept["wv"], 1)
            v.wait_ge(full["wv"], 2)
            v.tensor_copy(wbd_x[:, :, P:P + 2], ps[:, 6, 0:4].rearrange("p (c e) -> p c e", c=FB)).then_inc(kept["wv"], 1)
            for b in range(NB):
                v.wait_ge(full["xw"], b + 1)
                src = ps[:, 4 + b % 4, 0:FB * (P + 2)].rearrange("p (c e) -> p c e", c=FB)
                v.tensor_scalar(f2_half[:, b, :].rearrange("p (c e) -> p c e", c=FB), src[:, :, P:P + 2], 0.5, None,
                                ALU.mult).then_inc(f2_kept, 1)
                v.tensor_copy(yh[:, b, :].rearrange("p (c e) -> p c e", c=FB), src[:, :, 0:P]).then_inc(kept["xw"], 1)
            for n in range(2 * NC):
                v.wait_ge(full["f1"], 2 * NC + n + 1)
                v.tensor_copy(f1[:, 2 + n // NC, (n % NC) * CH:(n % NC + 1) * CH], ps[:, n, :]).then_inc(f1_late, 1)

            def mask(ps_no, pair):
                g0 = PASS * ps_no + PAIR * pair
                with v.Fori(0, NB // 2) as m:
                    for k in range(4):
                        row = adj_t[:, bass.ds(2 * m + k // 2, 1), :]
                        if ps_no == 0 and pair == 0 and k % 2 == 0:
                            v.wait_ge(adj_in[k // 2], 16 * m + 16)
                            v.tensor_copy(row, adj_row[:, k // 2:k // 2 + 1, :]).then_inc(adj_cast, 1)
                            v.wait_ge(adj_cast, 2 * m + (k // 2 + 1))
                        v.wait_ge(exp_done, 4 * m + (g0 + k + 1))
                        v.tensor_tensor(att[:, k:k + 1, :], att[:, k:k + 1, :], row, ALU.mult).then_inc(mask_done, 1)

            def take_heads(ps_no, pair):
                wid = D + 1
                v.wait_ge(att_free, 4 + PASS * ps_no + PAIR * (pair + 1))
                groups = [(h2, b3, PER_BANK * b3, min(NB - PER_BANK * b3, PER_BANK))
                          for h2 in range(2) for b3 in range(HEAD_BANKS)]

                def acc(h2, b3, cnt):
                    return ps[:, HEAD_BANKS * h2 + b3, 0:cnt * wid].rearrange("p (b e) -> p b e", e=wid)

                if ps_no == 0:
                    for h2, b3, i0, cnt in groups:
                        ins = v.tensor_scalar(sums[:, h2, i0:i0 + cnt], acc(h2, b3, cnt)[:, :, D], TINY, None, ALU.max)
                    step(ins)
                    step(v.reciprocal(rinv[:, 2 * pair:2 * pair + 2, :], sums[:]))
                for n, (h2, b3, i0, cnt) in enumerate(groups):
                    h = 2 * pair + h2
                    ins = v.tensor_tensor(nodes[:, i0:i0 + cnt, h * D:(h + 1) * D], acc(h2, b3, cnt)[:, :, 0:D],
                                          rinv[:, h, i0:i0 + cnt].unsqueeze(2).broadcast_to([P, cnt, D]), ALU.mult)
                ins.then_inc(acc_kept, 1)

            pows = 0

            def bn_measure(buf, k):
                i, c = divmod(k, FB)
                return v.bn_stats(bn_st[:, c, i, :], buf[:, c, i * CH:(i + 1) * CH])

            def batchnorm(buf, gain, shift, ins):
                nonlocal pows
                step(ins)
                for c in range(FB):
                    ins = v.bn_aggr(bn_mv[:, c, :], bn_st[:, c, :, :])
                step(ins)
                v.tensor_scalar(bn_ve[:], bn_mv[:, :, 1], EPS_BN, None, ALU.add).then_inc(var_ready, 1)
                pows += 1
                v.wait_ge(rstd_ready, pows)
                step(v.tensor_tensor(bn_a[:], bn_rs[:], par[:, gain, :], ALU.mult))
                step(v.tensor_tensor(bn_t[:], bn_mv[:, :, 0], bn_a[:], ALU.mult))
                step(v.tensor_tensor(bn_b[:], par[:, shift, :], bn_t[:], ALU.subtract))
                for c in range(FB):
                    v.tensor_scalar(buf[:, c, :], buf[:, c, :], bn_a[:, c:c + 1], bn_b[:, c:c + 1],
                                    ALU.mult, ALU.add).then_inc(bn_done, 1)

            elu_n = 0

            def elu_join(st, dst, residual, measure=False):
                nonlocal elu_n
                for k in range(8):
                    i, c = divmod(k, FB)
                    cols = dst[:, c, i * CH:(i + 1) * CH]
                    v.wait_ge(elu_e, elu_n + 1)
                    v.wait_ge(kept[st], k + 1)
                    v.scalar_tensor_tensor(cols, e_tmp[:, elu_n % 2, :], 1.0, r_tmp[:, elu_n % 2, :], ALU.min,
                                           ALU.add).then_inc(elu_free, 1)
                    elu_n += 1
                    v.wait_ge(elu_free, elu_n)
                    if residual is not None:
                        ins = v.scalar_tensor_tensor(cols, cols, -1.0, residual[:, c, i * CH:(i + 1) * CH], ALU.add, ALU.add)
                    else:
                        ins = v.tensor_scalar(cols, cols, -1.0, None, ALU.add)
                    ins.then_inc(elu_done, 1)
                    if measure and k:
                        v.wait_ge(elu_done, elu_n - 1)
                        bn_measure(dst, k - 1)
                if measure:
                    v.wait_ge(elu_done, elu_n)
                    return bn_measure(dst, 7)

            mask(0, 0)
            take_heads(0, 0)
            mask(0, 1)
            take_heads(0, 1)
            v.wait_ge(in_w, 64)
            for k in range(8):
                v.wait_ge(kept["xcT"], k + 1)
                last = bn_measure(feat_1, k)
            batchnorm(feat_1, G_ENC, B_ENC, last)
            last = elu_join("enc", feat_2, feat_1, measure=True)
            batchnorm(feat_2, G_ENC2, B_ENC2, last)
            mask(1, 0)
            take_heads(1, 0)
            v.wait_ge(full["deg"], NB)
            for l, add in enumerate((1.0, EPS_DEG)):
                for g in range(NG):
                    v.tensor_scalar(deg_ve[:, l, g, :], ps[:, 6, g * GB:(g + 1) * GB], add, None, ALU.add).then_inc(var_ready, 1)
            pows += 2 * NG
            mask(1, 1)
            take_heads(1, 1)
            elu_join("yw", feat_2, None)
            last = elu_join("dec", feat_1, feat_2, measure=True)
            batchnorm(feat_1, G_DEC, B_DEC, last)

            def ln_measure(ln, g, slot):
                wait_apart(ln_stats, g + (NG * ln + 1))
                for t in range(GB):
                    ins = v.bn_aggr(ln_mv[:, slot, t, :], ln_st[:, slot, t, :])
                ins.then_inc(ln_aggr, 1)
                v.wait_ge(ln_aggr, g + (NG * ln + 1))
                v.tensor_scalar(ln_ve[:, slot, :], ln_mv[:, slot, :, 1], EPS_LN, None, ALU.add).then_inc(ln_var, 1)

            def ln_apply(ln, g, slot):
                v.wait_ge(ln_rstd, g + (NG * ln + 1))
                for t in range(GB):
                    row = x_now[:, bass.ds(GB * g + t, 1), :]
                    ins = v.tensor_scalar(row, row, ln_mv[:, slot, t, 0:1], ln_rs[:, slot, t:t + 1],
                                          ALU.subtract, ALU.mult)
                ins.then_inc(ln_done, 1)

            def cut_scale(cut, ln, g, rem):
                v.wait_ge(ln_done, g + (NG * ln + 1))
                v.tensor_tensor(rem, x_now[:, bass.ds(GB * g, GB), :],
                                dinv[:, cut, bass.ds(g, 1), :].rearrange("p a b -> p (a b)").unsqueeze(2).broadcast_to([P, GB, F]),
                                ALU.mult).then_inc(cut_rest[0], 1)

            def cut_less(cut, g, s, rem):
                v.wait_ge(part_ready[s - 1], g + (NG * cut + 1))
                v.tensor_tensor(rem, rem, parts[cut][s - 1][:, bass.ds(GB * g, GB), :], ALU.subtract).then_inc(cut_rest[s], 1)

            for t in range(NG + 3):
                if t < NG:
                    for k in (2 * t, 2 * t + 1):
                        v.wait_ge(full["l0"], k + 1)
                        ins = v.tensor_tensor(x_now[:, 2 * k:2 * k + 2, :], ps[:, k, :].rearrange("p (b f) -> p b f", b=2),
                                              x_now[:, 2 * k:2 * k + 2, :], ALU.add)
                        ins.then_inc(kept["l0"], 1)
                    v.wait_ge(kept["l0"], 2 * t + 2)
                    for b in range(GB):
                        ins = v.bn_stats(ln_st[:, t % 2, b, :], x_now[:, GB * t + b, :])
                    ins.then_inc(ln_stats, 1)
                    ln_measure(0, t, t % 2)
                if 0 <= t - 1 < NG:
                    g = t - 1
                    ln_apply(0, g, g % 2)
                    cut_scale(0, 0, g, rest[0][:, g * GB:(g + 1) * GB, :])
                for s in (1, 2):
                    g = t - 1 - s
                    if 0 <= g < NG:
                        cut_less(0, g, s, rest[0][:, g * GB:(g + 1) * GB, :])

            def gcn_tail(layer, ln):
                with v.Fori(0, NG) as g:
                    for t in range(GB):
                        z = ps[:, 2 + t // 2:3 + t // 2, (t % 2) * F:(t % 2) * F + F]
                        row = nodes[:, bass.ds(GB * g + t, 1), :]
                        d = dinv[:, layer, bass.ds(g, 1), t]
                        if t % 2 == 0:
                            v.wait_ge(full["z"], 2 * g + (8 * layer + t // 2 + 3))
                        if layer:
                            ins = v.scalar_tensor_tensor(row, z, d, row_s[:, 1:2, :], ALU.mult, ALU.add)
                        else:
                            ins = v.tensor_scalar(row, z, d, 0.0, ALU.mult, ALU.max)
                        if t % 2:
                            ins.then_inc(kept["z"], 1)
                    v.wait_ge(kept["z"], 2 * g + (8 * layer + 2 + 2))
                    rows_g = x_now[:, bass.ds(GB * g, GB), :]
                    v.tensor_tensor(rows_g, rows_g, nodes[:, bass.ds(GB * g, GB), :], ALU.add).then_inc(z_added, 1)
                    wait_apart(z_added, g + (NG * layer + 1))
                    for t in range(GB):
                        ins = v.bn_stats(ln_st[:, 0:1, t, :], x_now[:, bass.ds(GB * g + t, 1), :])
                    ins.then_inc(ln_stats, 1)
                    ln_measure(ln, g, 0)
                    ln_apply(ln, g, 0)

            gcn_tail(0, 1)

            for k in range(16):
                i, c = divmod(k % 8, FB)
                dst = (feat_2 if k < 8 else feat_3)[:, c, i * CH:(i + 1) * CH]
                v.wait_ge(full["qk"], k + 1)
                if k < 8:
                    ins = v.tensor_scalar(dst, ps[:, k % 8, :], par[:, BIAS_Q, c:c + 1], 1.0 / 16, ALU.add, ALU.mult)
                else:
                    ins = v.tensor_scalar(dst, ps[:, k % 8, :], par[:, BIAS_K, c:c + 1], None, ALU.add)
                ins.then_inc(kept["qk"], 1)
            for k in range(8):
                v.wait_ge(full["v"], k + 1)
                v.tensor_tensor(nodes[:, 2 * k:2 * k + 2, :], ps[:, k, :].rearrange("p (b f) -> p b f", b=2),
                                row_s[:, 0:1, :].broadcast_to([P, 2, F]), ALU.add).then_inc(kept["v"], 1)

            def row_max(ib, b):
                v.wait_ge(s_full, ib + 1)
                v.tensor_reduce(neg_max[:, b:b + 1], ps[:, 0:4, :], AX.XY, ALU.max, negate=True).then_inc(max_ready, 1)

            def tail(ib, b):
                for q, bank in ((1, 5), (3, 4)):
                    v.wait_ge(t_full, 4 * ib + (q + 1))
                    v.tensor_copy(prob_t[:, b, q * BPC:(q + 1) * BPC, :],
                                  ps[:, bank, :].rearrange("p (k i) -> p k i", k=BPC)).then_inc(t_dve, 1)

            def finish(ib, t):
                v.wait_ge(p_ready, ib + 1)
                v.reciprocal(row_inv[:, bass.ds(ib, 1)], row_sum[:, bass.ds(ib, 1)]).then_inc(inv_ready, 1)
                v.wait_ge(o_full, ib + 1)
                v.wait_ge(inv_ready, ib + 1)
                v.scalar_tensor_tensor(x_now[:, bass.ds(ib, 1), :], ps[:, 7:8, 0:F], row_inv[:, bass.ds(ib, 1)],
                                       x_now[:, bass.ds(ib, 1), :], ALU.mult, ALU.add).then_inc(o_kept, 1)
                wait_apart(o_kept, ib + 1)
                ins = v.bn_stats(ln_st[:, 0:1, t, :], x_now[:, bass.ds(ib, 1), :])
                if t == GB - 1:
                    ins.then_inc(ln_stats, 1)

            def attend_group(g):
                for t in range(GB):
                    tail(GB * g + t, t % 2)
                    if not (isinstance(g, int) and t == GB - 1):
                        row_max(GB * g + (t + 1), (t + 1) % 2)
                    finish(GB * g + t, t)
                ln_measure(2, g, 0)
                ln_apply(2, g, 0)
                cut_scale(1, 2, g, rest[1])
                for s in range(3):
                    if s:
                        cut_less(1, g, s, rest[1])
                    v.wait_ge(cut_rest[s], g + (NG + 1))
                    v.tensor_copy(parts[1][s][:, bass.ds(GB * g, GB), :], rest[1]).then_inc(part_ready[s], 1)

            row_max(0, 0)
            with v.Fori(0, NG - 1) as g:
                attend_group(g)
            attend_group(NG - 1)
            gcn_tail(1, 3)

        @block.tensor
        def _(pe):
            def feature_product(st, w, src, first=lambda k: None):
                for i in range(NC):
                    for e in range(FB):
                        k = i * FB + e
                        first(k)
                        for f in range(FB):
                            mm = pe.matmul(ps[:, k, :], w_all[:, w, f, e * P:(e + 1) * P],
                                           src[:, f, i * CH:(i + 1) * CH], start=f == 0, stop=f == FB - 1)
                        mm.then_inc(full[st], 1)

            def node_product(st, w, src, first=lambda k: None):
                for k in range(8):
                    first(k)
                    for b in (2 * k, 2 * k + 1):
                        o = (b % 2) * F
                        for f in range(FB):
                            mm = pe.matmul(ps[:, k, o:o + F], src[:, f, b * P:(b + 1) * P],
                                           w_all[:, w, f, :], start=f == 0, stop=f == FB - 1)
                    mm.then_inc(full[st], 1)

            def to_features(st, src, first=lambda k: None):
                for i in range(NC):
                    for c in range(FB):
                        first(i * FB + c)
                        for t in range(BPC):
                            mm = pe.transpose(ps[:, i * FB + c, t * P:(t + 1) * P],
                                              src[:, i * BPC + t, c * P:(c + 1) * P], ident[:])
                        mm.then_inc(full[st], 1)

            def to_nodes(st, src, first=lambda k: None):
                for k in range(8):
                    first(k)
                    for b in (2 * k, 2 * k + 1):
                        for c in range(FB):
                            mm = pe.transpose(ps[:, k, (b % 2) * F + c * P:(b % 2) * F + (c + 1) * P],
                                              src[:, c, b * P:(b + 1) * P], ident[:])
                    mm.then_inc(full[st], 1)

            pe.wait_ge(in_h, 64)
            for h in range(H):
                mm = pe.matmul(ps[:, 7, h * P:(h + 1) * P], wtbd_s[:, h // 2, :], v0_s[:, h, :], start=True, stop=True)
            mm.then_inc(full["wv"], 1)
            for c in range(FB):
                mm = pe.matmul(ps[:, 6, 2 * c:2 * c + 2], wtbd_s[:, c, :], v1_s[:, c, :], start=True, stop=True)
            mm.then_inc(full["wv"], 1)
            pe.wait_ge(in_x, 32)
            pe.wait_ge(kept["wv"], 1)

            def f1_head(h, bank, first):
                for i in range(NC):
                    first(i)
                    pe.matmul(ps[:, bank + i, :], wv0_s[:, h, :], x_t[:, h // 2, i * CH:(i + 1) * CH],
                              start=True, stop=True).then_inc(full["f1"], 1)

            f1_head(0, 0, lambda i: None)
            f1_head(1, 0, lambda i: pe.wait_ge(kept["f1"], i + 1))
            pe.wait_ge(kept["wv"], 2)
            for b in range(NB):
                if b >= 4:
                    pe.wait_ge(kept["xw"], b - 3)
                for c in range(FB):
                    mm = pe.matmul(ps[:, 4 + b % 4, c * (P + 2):(c + 1) * (P + 2)], x_t[:, c, b * P:(b + 1) * P],
                                   wbd_x[:, c, :], start=True, stop=True)
                mm.then_inc(full["xw"], 1)
            f1_head(2, 0, lambda i: pe.wait_ge(kept["f1"], NC + i + 1))
            f1_head(3, 4, lambda i: pe.wait_ge(kept["xw"], NB - 3 + i))

            def attend(ps_no, pair):
                wid = D + 1
                n = 2 * ps_no + pair
                g0 = PASS * ps_no + PAIR * pair
                if n:
                    pe.wait_ge(acc_kept, n)
                for b in range(2 * HEAD_BANKS):
                    pe.matmul(ps[:, b, :], zeros_b[:, 0:P], zeros_b[:], start=True, stop=True, skip_group_check=True)
                with pe.Fori(0, NB // 2) as m:
                    for k in range(4):
                        pe.wait_ge(mask_done, 4 * m + (g0 + k + 1))
                        pe.wait_ge(mov_ready, 4 * m + (g0 + k + 1))
                        for b in range(NB):
                            o = (b % PER_BANK) * wid
                            mm = pe.matmul(ps[:, HEAD_BANKS * (k % 2) + b // PER_BANK, o:o + MOVING],
                                           att[:, k, b * P:(b + 1) * P], mov_s[:, k, :],
                                           start=False, stop=True, skip_group_check=True)
                        mm.then_inc(att_free, 1)
                    if n == 2:
                        for u in range(2):
                            for j in range(NB):
                                mm = pe.matmul(ps[:, 6, bass.ds(2 * m + u, 1)], adj_t[:, j, bass.ds((2 * m + u) * P, P)],
                                               ones_b[:], start=j == 0, stop=j == NB - 1)
                            mm.then_inc(full["deg"], 1)

            pe.wait_ge(consts, 6)
            pe.wait_ge(f1_late, 2 * NC)
            attend(0, 0)
            attend(0, 1)
            pe.wait_ge(acc_kept, 2)
            to_features("xcT", nodes)
            pe.wait_ge(in_w, 64)
            pe.wait_ge(kept["xcT"], 8)
            pe.wait_ge(bn_done, 2)
            feature_product("enc", W_ENC, feat_1)
            pe.wait_ge(bn_done, 4)
            to_nodes("emb", feat_2, first=lambda k: pe.wait_ge(kept["enc"], k + 1))
            pe.wait_ge(kept["emb"], 8)
            attend(1, 0)
            attend(1, 1)
            pe.wait_ge(acc_kept, 4)
            to_features("yT", nodes)
            for i in range(NC):
                for c in range(FB):
                    pe.wait_ge(kept["yT"], i * FB + c + 1)
                    pe.matmul(ps[:, i * FB + c, :], wtbd_s[:, c, :], feat_1[:, c, i * CH:(i + 1) * CH],
                              start=True, stop=True).then_inc(full["yw"], 1)

            def dec_ready(k):
                pe.wait_ge(kept["yw"], k + 1)
                pe.wait_ge(elu_done, 8 + FB * (k // FB + 1))

            feature_product("dec", W_DEC, feat_2, first=dec_ready)
            pe.wait_ge(bn_done, 6)
            to_nodes("l0", feat_1, first=lambda k: pe.wait_ge(kept["dec"], k + 1))

            def gcn(layer, w, self_loops):
                with pe.Fori(0, NC) as m:
                    for c in range(FB):
                        cols = slice(c * P, (c + 1) * P)
                        pe.wait_ge(kept["ax"], FB * m + (8 * layer + c + 1))
                        for g in range(NG):
                            for s in range(3):
                                pe.wait_ge(part_ready[s], NG * layer + g + 1)
                                for j in range(g * GB, (g + 1) * GB):
                                    mm = pe.matmul(ps[:, c, :], parts[layer][s][:, j, cols],
                                                   adj_t[:, j, bass.ds(m * CH, CH)], start=g == 0 and s == 0 and j == 0,
                                                   stop=j == NB - 1 and s == 2 and not self_loops, skip_group_check=True)
                        if self_loops:
                            for s in range(3):
                                for t in range(BPC):
                                    mm = pe.matmul(ps[:, c, t * P:(t + 1) * P],
                                                   parts[layer][s][:, bass.ds(m * BPC + t, 1), cols], eye_b[:],
                                                   start=False, stop=s == 2, skip_group_check=True)
                        mm.then_inc(full["ax"], 1)
                    pe.wait_ge(kept["ax"], FB * m + (8 * layer + 2 + 2))
                    for k in range(2):
                        pe.wait_ge(kept["z"], 2 * m + (8 * layer + k + 1))
                        for b in (2 * k, 2 * k + 1):
                            for f in range(FB):
                                mm = pe.matmul(ps[:, 2 + k, (b % 2) * F:(b % 2) * F + F], ax_chunk[:, f, b * P:(b + 1) * P],
                                               w_all[:, w, f, :], start=f == 0, stop=f == FB - 1)
                        mm.then_inc(full["z"], 1)

            pe.wait_ge(kept["l0"], 8)
            gcn(0, W_L1, True)

            def x2_ready(k):
                pe.wait_ge(kept["z"], 8 + 2)
                pe.wait_ge(ln_done, NG + k // FB + 1)

            to_features("x2T", x_now, first=x2_ready)
            pe.wait_ge(kept["x2T"], 8)
            feature_product("qk", W_Q, feat_1)
            feature_product("qk", W_K, feat_1, first=lambda k: pe.wait_ge(kept["qk"], k + 1))
            node_product("v", W_V, feat_1, first=lambda k: pe.wait_ge(kept["qk"], 8 + k + 1))
            pe.wait_ge(kept["v"], 8)

            def scores(ib, b, free):
                pe.wait_ge(q_ready, ib + 1)
                if free:
                    pe.wait_ge(p_ready, ib)
                for jc in range(NC):
                    for f in range(FB):
                        pe.matmul(ps[:, jc, :], q_blk[:, b, f, :], feat_3[:, f, jc * CH:(jc + 1) * CH],
                                  start=f == 0, stop=False, skip_group_check=True)
                    for t in range(BPC):
                        mm = pe.matmul(ps[:, jc, t * P:(t + 1) * P], adj_t[:, jc * BPC + t, bass.ds(ib * P, P)],
                                       two_b[:], start=False, stop=True, skip_group_check=True)
                mm.then_inc(s_full, 1)

            def values(ib, b, first=False):
                pe.wait_ge(p_ready, ib + 1)
                for q, bank in enumerate((4, 5, 6, 4)):
                    if q == 3:
                        pe.wait_ge(t_act, 2 * ib + 1)
                    elif not first:
                        if q == 1:
                            pe.wait_ge(t_dve, 2 * ib - 1)
                        elif q == 0:
                            pe.wait_ge(t_dve, 2 * ib)
                        else:
                            pe.wait_ge(t_act, 2 * ib)
                    for t in range(BPC):
                        j = q * BPC + t
                        mm = pe.transpose(ps[:, bank, t * P:(t + 1) * P], prob[:, b, j * P:(j + 1) * P], ident[:])
                    mm.then_inc(t_full, 1)
                if not first:
                    pe.wait_ge(o_kept, ib)
                for q in range(NC):
                    pe.wait_ge(t_act if q % 2 == 0 else t_dve, 2 * ib + (q // 2 + 1))
                    for t in range(BPC):
                        j = q * BPC + t
                        mm = pe.matmul(ps[:, 7, 0:F], prob_t[:, b, j, :], nodes[:, j, :],
                                       start=j == 0, stop=j == NB - 1)
                mm.then_inc(o_full, 1)

            scores(0, 0, False)
            scores(1, 1, True)
            values(0, 0, first=True)
            with pe.Fori(0, NB // 2 - 1) as m:
                scores(2 * m + 2, 0, True)
                values(2 * m + 1, 1)
                scores(2 * m + 3, 1, True)
                values(2 * m + 2, 0)
            values(NB - 1, 1)

            pe.wait_ge(o_kept, NB)
            gcn(1, W_L3, False)


def kernel(x, adj, L0_gnn_W, L0_gnn_V, L0_gnn_enc_bn_gamma, L0_gnn_enc_bn_beta, L0_gnn_enc_mlp_W,
           L0_gnn_enc_mlp_b, L0_gnn_enc_mlp_bn_gamma, L0_gnn_enc_mlp_bn_beta, L0_gnn_dec_mlp_W,
           L0_gnn_dec_mlp_b, L0_gnn_dec_mlp_bn_gamma, L0_gnn_dec_mlp_bn_beta, L1_gnn_W,
           L2_gnn_Wq, L2_gnn_bq, L2_gnn_Wk, L2_gnn_bk, L2_gnn_Wv, L2_gnn_bv, L3_gnn_W, L3_gnn_b):
    import numpy as np
    import concourse.bacc as bacc
    from concourse.bass_utils import run_bass_kernel_spmd

    W, V = np.asarray(L0_gnn_W), np.asarray(L0_gnn_V)
    wbd = np.zeros((FB, P, P), W.dtype)
    wtbd = np.zeros((FB, P, P), W.dtype)
    v0rep = np.zeros((H, P, P), V.dtype)
    v1 = np.zeros((FB, P, 2), V.dtype)
    for h in range(H):
        c, r = divmod(h, 2)
        rows = slice(r * D, (r + 1) * D)
        wbd[c, rows, rows] = W[h]
        wtbd[c, rows, rows] = W[h].T
        v0rep[h, rows, :] = V[h, 0]
        v1[c, rows, r] = V[h, 1, :, 0]

    def blocks(w):
        return np.asarray(w).reshape(FB, P, F).transpose(1, 0, 2)

    weights = np.stack([blocks(np.asarray(L0_gnn_enc_mlp_W).T), blocks(np.asarray(L0_gnn_dec_mlp_W).T),
                        blocks(L1_gnn_W), blocks(L2_gnn_Wq), blocks(L2_gnn_Wk), blocks(L2_gnn_Wv),
                        blocks(np.asarray(L3_gnn_W).T)], axis=1)
    params = np.stack([np.asarray(a).reshape(FB, P).T for a in (
        L0_gnn_enc_bn_gamma, L0_gnn_enc_bn_beta, L0_gnn_enc_mlp_b, L0_gnn_enc_mlp_bn_gamma,
        L0_gnn_enc_mlp_bn_beta, L0_gnn_dec_mlp_b, L0_gnn_dec_mlp_bn_gamma, L0_gnn_dec_mlp_bn_beta,
        L2_gnn_bq, L2_gnn_bk)], axis=1)
    rows = np.stack([np.broadcast_to(np.asarray(a), (P, F)) for a in (L2_gnn_bv, L3_gnn_b)], axis=1)
    x, adj = np.asarray(x), np.asarray(adj)
    arrays = {k: np.ascontiguousarray(a) for k, a in dict(
        x=x, xT=x.T, adjT=adj.T, wbd=wbd, wtbd=wtbd, v0rep=v0rep, v1=v1, weights=weights,
        params=params, rows=rows).items()}

    nc = bacc.Bacc("TRN2", target_bir_lowering=False, num_devices=1)
    aps = {k: nc.dram_tensor("in_" + k, a.shape, mybir.dt.from_np(a.dtype), kind="ExternalInput").ap()
           for k, a in arrays.items()}
    out = nc.dram_tensor("out", (N, F), F32, kind="ExternalOutput").ap()
    gnn_stack(nc, out=out, **aps)
    r = run_bass_kernel_spmd(nc, [{"in_" + k: a for k, a in arrays.items()}], core_ids=[0])
    return r.results[0]["out"]
```

```python
from contextlib import ExitStack

import concourse.bass as bass
from concourse import mybir

ACT = mybir.ActivationFunctionType
ALU = mybir.AluOpType
AX = mybir.AxisListType
F32 = mybir.dt.float32
BF16 = mybir.dt.bfloat16

P = 128
N = 2048
F = 256
H = 4
D = F // H
NB = N // P
FB = F // P
CH = 512
NC = N // CH
BPC = CH // P
EPS_BN = 1e-6
EPS_LN = 1e-5
EPS_DEG = 1e-8
MOVING = 96
GB = BPC
NG = NB // GB
TINY = 1e-30
PER_BANK = 6
HEAD_BANKS = 3

W_ENC, W_DEC, W_L1, W_Q, W_K, W_V, W_L3 = range(7)
G_ENC, B_ENC, BIAS_ENC, G_ENC2, B_ENC2, BIAS_DEC, G_DEC, B_DEC, BIAS_Q, BIAS_K = range(10)


def gnn_stack(nc, x, xT, adjT, wbd, wtbd, v0rep, v1, weights, params, rows, out):
    with ExitStack() as ctx:
        def sb(name, shape, dt=F32):
            return ctx.enter_context(nc.sbuf_tensor(name, shape, dt))

        def sem(name):
            return ctx.enter_context(nc.semaphore(name))

        adj_t = sb("adj_t", [P, NB, N], BF16)
        f1_all = sb("f1_all", [P, H * N])
        big = sb("big", [P, 4 * N])
        node_b = sb("node_b", [P, NB * F])
        node_a = sb("node_a", [P, NB * F])
        x_now = sb("x_now", [P, NB, F])
        w_all = sb("w_all", [P, 7, FB, F])
        wtbd_s = sb("wtbd_s", [P, FB, P])
        v0_s = sb("v0_s", [P, H, P])
        v1_s = sb("v1_s", [P, FB, 2])
        par = sb("par", [P, 10, FB])
        row_s = sb("row_s", [P, 2, F])
        ident = sb("ident", [P, P])
        credit = sb("credit", [P, 3])
        pause = sb("pause", [P, 1])
        eye_b = sb("eye_b", [P, P], BF16)
        two_b = sb("two_b", [P, P], BF16)
        zeros_b = sb("zeros_b", [P, CH], BF16)
        ones_b = sb("ones_b", [P, P], BF16)
        minus_half = sb("minus_half", [P, GB])
        wv0_s = sb("wv0_s", [P, H, P])
        wbd_x = sb("wbd_x", [P, FB, P + 2])
        mov_s = sb("mov_s", [P, 4, MOVING])
        f2_half = sb("f2_half", [P, NB, H])
        deg = sb("deg", [P, NB])
        deg_ve = sb("deg_ve", [P, 2, NG, GB])
        dinv = sb("dinv", [P, 2, NG, GB])
        sums = sb("sums", [P, 2, NB])
        rinv = sb("rinv", [P, H, NB])
        bn_st = sb("bn_st", [P, FB, NC, 6])
        bn_mv = sb("bn_mv", [P, FB, 2])
        bn_ve = sb("bn_ve", [P, FB])
        bn_rs = sb("bn_rs", [P, FB])
        bn_a = sb("bn_a", [P, FB])
        bn_b = sb("bn_b", [P, FB])
        ln_st = sb("ln_st", [P, 2, GB, 6])
        ln_mv = sb("ln_mv", [P, 2, GB, 2])
        ln_ve = sb("ln_ve", [P, 2, GB])
        ln_rs = sb("ln_rs", [P, 2, GB])
        ln_shift = sb("ln_shift", [P, 2, GB])
        q_blk = sb("q_blk", [P, 2, FB, P])
        neg_max = sb("neg_max", [P, 2])
        row_sum = sb("row_sum", [P, NB])
        row_inv = sb("row_inv", [P, NB])

        feat_1 = big[:, 0:2 * N].rearrange("p (c n) -> p c n", c=FB)
        feat_2 = big[:, 2 * N:4 * N].rearrange("p (c n) -> p c n", c=FB)
        att = big[:, :].rearrange("p (k n) -> p k n", k=4)
        x_t = x_now[:, :, :].rearrange("p b f -> p (b f)").rearrange("p (c n) -> p c n", c=FB)
        early = x_now[:, :, :].rearrange("p b f -> p (b f)").rearrange("p (k n) -> p k n", k=2)
        yh = node_b[:, :].rearrange("p (b f) -> p b f", b=NB)
        feat_3 = node_b[:, :].rearrange("p (c n) -> p c n", c=FB)
        e_tmp = node_b[:, 0:2 * CH].rearrange("p (k n) -> p k n", k=2)
        r_tmp = node_b[:, 2 * CH:4 * CH].rearrange("p (k n) -> p k n", k=2)
        ax_chunk = node_b[:, 0:FB * CH].rearrange("p (c n) -> p c n", c=FB)
        nodes = node_a[:, :].rearrange("p (b f) -> p b f", b=NB)
        adj_row = node_a[:, :].rearrange("p (k n) -> p k n", k=2)
        f1 = f1_all[:, :].rearrange("p (h n) -> p h n", h=H)
        prob = f1_all[:, 0:2 * N].rearrange("p (k n) -> p k n", k=2)
        prob_t = f1_all[:, 2 * N:4 * N].rearrange("p (k b i) -> p k b i", k=2, b=NB)
        w_flat = w_all[:, :, :, :].rearrange("p w c f -> p (w c f)")

        def bf16_nodes(words):
            return words.bitcast(BF16).rearrange("p (b f) -> p b f", b=NB)

        half = NB * F // 2
        parts = [[bf16_nodes(big[:, s * half:(s + 1) * half]) for s in range(3)],
                 [bf16_nodes(big[:, 0:half]), bf16_nodes(big[:, half:2 * half]), bf16_nodes(w_flat[:, 0:half])]]
        rest = [nodes, w_flat[:, half:half + GB * F].rearrange("p (b f) -> p b f", b=GB)]

        deg_rows = [t[:, :, :].rearrange("p a b -> p (a b)") for t in (v0_s, wv0_s)] \
            + [q_blk[:, :, :, :].rearrange("p a b c -> p (a b c)")]

        adj_flat = adj_t[:, :, :].rearrange("p b i -> p (b i)")
        diagonal = [adj_flat[:, 0:(NB - 1) * (N + P)].rearrange("p (b i) -> p b i", i=N + P)[:, :, 0:P],
                    adj_flat[:, (NB - 1) * (N + P):].unsqueeze(1)]

        ps = ctx.enter_context(nc.psum_tensor("ps", [P, 8, CH], F32))

        in_x = sem("in_x")
        in_h = sem("in_h")
        in_w = sem("in_w")
        in_res = sem("in_res")
        adj_in = [sem("adj_in0"), sem("adj_in1")]
        adj_cast = sem("adj_cast")
        consts = sem("consts")
        const_a = sem("const_a")
        full = {}
        kept = {}
        for st in ("wv", "f1", "xw", "deg", "xcT", "enc", "emb", "yT", "yw", "dec", "l0",
                   "ax", "z", "x2T", "qk", "v"):
            full[st] = sem("full_" + st)
            kept[st] = sem("kept_" + st)
        f1_late = sem("f1_late")
        emb_late = sem("emb_late")
        f2_kept = sem("f2_kept")
        elu_e = sem("elu_e")
        elu_free = sem("elu_free")
        elu_done = sem("elu_done")
        dve = sem("dve")
        tanh_done = sem("tanh_done")
        exp_done = sem("exp_done")
        mask_done = sem("mask_done")
        mov_ready = sem("mov_ready")
        att_free = sem("att_free")
        acc_kept = sem("acc_kept")
        var_ready = sem("var_ready")
        rstd_ready = sem("rstd_ready")
        bn_done = sem("bn_done")
        ln_stats = sem("ln_stats")
        ln_aggr = sem("ln_aggr")
        ln_var = sem("ln_var")
        ln_rstd = sem("ln_rstd")
        ln_shift_ready = sem("ln_shift_ready")
        ln_done = sem("ln_done")
        loops_set = sem("loops_set")
        z_added = sem("z_added")
        biased = sem("biased")
        cut_rest = [sem(f"cut_rest{s}") for s in range(3)]
        part_ready = [sem(f"part_ready{s}") for s in range(3)]
        q_ready = sem("q_ready")
        s_full = sem("s_full")
        max_ready = sem("max_ready")
        p_ready = sem("p_ready")
        t_full = sem("t_full")
        t_act = sem("t_act")
        t_dve = sem("t_dve")
        o_full = sem("o_full")
        o_kept = sem("o_kept")
        inv_ready = sem("inv_ready")
        out_done = sem("out_done")

        def att_tile(ps_no, pair, m, k):
            if ps_no and not pair and isinstance(m, int) and m == 0 and k < 2:
                return early[:, k:k + 1, :]
            slot = (k + 2 * ps_no) % 4
            return att[:, slot:slot + 1, :]

        def chunk_bank(i):
            return FB * ((i + 2) % NC)

        def xw_bank(b):
            return b % 4 if b else 4

        PAIR = 2 * NB
        PASS = 2 * PAIR
        block = ctx.enter_context(nc.Block())

        @block.sync
        def _(sp):
            sp.dma_start(wtbd_s[:], wtbd.rearrange("c p e -> p c e")).then_inc(in_h, 16)
            sp.dma_start(v0_s[:], v0rep.rearrange("h p e -> p h e")).then_inc(in_h, 16)
            for c in range(FB):
                sp.dma_start(x_t[:, c, :], xT[c * P:(c + 1) * P, :]).then_inc(in_x, 16)
            for s in range(2):
                sp.dma_start(adj_row[:, s, :], adjT[s * P:(s + 1) * P, :]).then_inc(adj_in[s], 16)
            with sp.Fori(1, NB // 2) as m:
                for s in range(2):
                    sp.wait_ge(adj_cast, 2 * m + s - 1)
                    sp.dma_start(adj_row[:, s, :], adjT[bass.ds((2 * m + s) * P, P), :]).then_inc(adj_in[s], 16)
            sp.wait_ge(att_free, 4 + PASS + 2)
            sp.dma_start(x_now[:], x.rearrange("(b p) f -> p b f", p=P)).then_inc(in_res, 16)
            out_v = out.rearrange("(b p) f -> p b f", p=P)
            with sp.Fori(0, NG) as g:
                sp.wait_ge(ln_done, g + (3 * NG + 1))
                sp.dma_start(out_v[:, bass.ds(g * GB, GB), :], x_now[:, bass.ds(g * GB, GB), :]).then_inc(out_done, 16)
            sp.wait_ge(out_done, 16 * NG)

        @block.gpsimd
        def _(pool):
            pool.memset(ident[:], 0.0).then_inc(const_a, 1)
            pool.memset(eye_b[:], 0.0).then_inc(const_a, 1)
            pool.memset(two_b[:], 0.0).then_inc(const_a, 1)
            pool.memset(zeros_b[:], 0.0).then_inc(consts, 1)
            pool.memset(ones_b[:], 1.0).then_inc(att_free, 4)
            pool.memset(mov_s[:, :, D:D + 1], 1.0).then_inc(consts, 1)
            pool.memset(mov_s[:, :, D + 1:MOVING], 0.0).then_inc(consts, 1)
            for n, (s_, c) in enumerate(((kept["ax"], 2), (kept["z"], 2), (full["z"], 2))):
                pool.memset(credit[:, n:n + 1], 0.0).then_inc(s_, c)
            pool.memset(minus_half[:], -0.5).then_inc(const_a, 1)
            pool.wait_ge(const_a, 4)
            for m, v in ((ident, 1.0), (eye_b, 1.0), (two_b, 2.0)):
                pool.affine_select(out=m[:], in_=m[:], compare_op=ALU.not_equal, fill=v, base=0,
                                   pattern=[[-1, P]], channel_multiplier=1).then_inc(consts, 1)

            def moving(ps_no, pair):
                g0 = PASS * ps_no + PAIR * pair
                with pool.Fori(0, NB // 2) as m:
                    for k in range(4):
                        if g0 == 0:
                            pool.wait_ge(kept["xw"], 2 * m + (k // 2 + 1))
                        h = 2 * pair + k % 2
                        pool.wait_ge(att_free, 4 * m + (g0 + k + 1))
                        pool.tensor_copy(mov_s[:, k:k + 1, 0:D], yh[:, bass.ds(2 * m + k // 2, 1), h * D:(h + 1) * D])\
                            .then_inc(mov_ready, 1)

            n = 0

            def power(dst, src, width):
                nonlocal n
                n += 1
                pool.wait_ge(var_ready, n)
                pool.tensor_tensor(dst, src, minus_half[:, 0:width], ALU.pow).then_inc(rstd_ready, 1)

            def ln_power(ln, g, slot):
                pool.wait_ge(ln_var, g + (NG * ln + 1))
                pool.tensor_tensor(ln_rs[:, slot, :], ln_ve[:, slot, :], minus_half[:], ALU.pow).then_inc(ln_rstd, 1)

            moving(0, 0)
            moving(0, 1)
            power(bn_rs[:], bn_ve[:], FB)
            power(bn_rs[:], bn_ve[:], FB)
            pool.wait_ge(kept["emb"], 4)
            pool.wait_ge(emb_late, 4)
            moving(1, 0)
            moving(1, 1)
            for g, l in ((g, l) for g in range(NG) for l in range(2)):
                power(dinv[:, l, g, :], deg_ve[:, l, g, :], GB)
            power(bn_rs[:], bn_ve[:], FB)
            for g in range(NG):
                ln_power(0, g, g % 2)
            with pool.Fori(0, NG) as g:
                ln_power(1, g, 0)

            pool.wait_ge(kept["qk"], 8)
            for b in range(2):
                pool.tensor_copy(q_blk[:, b], feat_2[:, :, b * P:(b + 1) * P]).then_inc(q_ready, 1)

            def q_copies(g):
                for t in range(GB):
                    if isinstance(g, int) and g * GB + t + 2 >= NB:
                        continue
                    pool.wait_ge(s_full, GB * g + (t + 1))
                    pool.tensor_copy(q_blk[:, t % 2], feat_2[:, :, bass.ds((GB * g + (t + 2)) * P, P)]).then_inc(q_ready, 1)

            with pool.Fori(0, NG - 1) as g:
                q_copies(g)
                ln_power(2, g, 0)
            q_copies(NG - 1)
            ln_power(2, NG - 1, 0)
            with pool.Fori(0, NG) as g:
                ln_power(3, g, 0)

        @block.scalar
        def _(act):
            act.dma_start(v1_s[:], v1.rearrange("c p e -> p c e")).then_inc(in_h, 16)
            act.dma_start(wbd_x[:, :, 0:P], wbd.rearrange("c p e -> p c e")).then_inc(in_h, 16)

            def drain(st, dsts):
                for k, (dst, src) in enumerate(dsts):
                    act.wait_ge(full[st], k + 1)
                    act.activation(dst, src, ACT.Copy).then_inc(kept[st], 1)

            def head_dst(buf):
                return [(buf[:, c, i * CH:(i + 1) * CH], ps[:, c * NC + i, :]) for c in range(FB) for i in range(NC)]

            def keep_f1(h):
                for i in range(NC):
                    act.wait_ge(full["f1"], NC * h + i + 1)
                    act.activation(f1[:, h, i * CH:(i + 1) * CH], ps[:, NC * h + i, :], ACT.Copy).then_inc(kept["f1"], 1)

            keep_f1(0)

            def attention(ps_no, pair, between=None):
                g0 = PASS * ps_no + PAIR * pair

                def tanhs(m, k, free=False):
                    for t in (k, k + 1):
                        if g0 == 0 and isinstance(m, int) and k == 0:
                            if t:
                                keep_f1(1)
                            act.wait_ge(kept["f1"], NC * (t + 1))
                        h = 2 * pair + t % 2
                        if not free:
                            act.wait_ge(att_free, 4 * m + (g0 + t + 1))
                        if g0 == 0:
                            act.wait_ge(f2_kept, 2 * m + (k // 2 + 1))
                        act.activation(att_tile(ps_no, pair, m, t), f1[:, h:h + 1, :], ACT.Tanh, scale=0.5,
                                       bias=f2_half[:, bass.ds(2 * m + k // 2, 1), h]).then_inc(tanh_done, 1)

                def expo(m, t):
                    act.wait_ge(tanh_done, 4 * m + (g0 + t + 1))
                    tile = att_tile(ps_no, pair, m, t)
                    act.activation(tile, tile, ACT.Exp, scale=0.5).then_inc(exp_done, 1)

                def two_tiles(m, k, free=False):
                    tanhs(m, k, free)
                    expo(m, k)
                    expo(m, k + 1)

                start = 0
                if g0 == 0:
                    two_tiles(0, 0)
                    two_tiles(0, 2)
                    start = 1
                if between is not None:
                    two_tiles(0, 0, free=True)
                    between[0]()
                    tanhs(0, 2, free=True)
                    between[1]()
                    expo(0, 2)
                    between[2]()
                    expo(0, 3)
                    two_tiles(1, 0, free=True)
                    two_tiles(1, 2)
                    start = 2
                with act.Fori(start, NB // 2) as m:
                    two_tiles(m, 0)
                    two_tiles(m, 2)

            attention(0, 0)
            act.wait_ge(full["f1"], H * NC)
            act.wait_ge(full["xw"], NB)
            act.dma_start(par[:], params).then_inc(in_w, 16)
            act.dma_start(w_all[:], weights).then_inc(in_w, 16)
            act.dma_start(row_s[:], rows).then_inc(in_w, 16)
            act.wait_ge(f1_late, 2 * NC)
            attention(0, 1)

            elu_n = 0

            def elu_parts(st, bias):
                nonlocal elu_n
                for k in range(8):
                    b = par[:, bias, k % FB:k % FB + 1] if bias is not None else 0.0
                    act.wait_ge(full[st], k + 1)
                    if elu_n >= 2:
                        act.wait_ge(elu_free, elu_n - 1)
                    act.activation(e_tmp[:, elu_n % 2, :], ps[:, k, :], ACT.Exp, bias=b).then_inc(elu_e, 1)
                    act.activation(r_tmp[:, elu_n % 2, :], ps[:, k, :], ACT.Relu, bias=b).then_inc(kept[st], 1)
                    elu_n += 1

            def keep_degrees(chunk, bank):
                act.wait_ge(full["deg"], chunk + 1)
                act.activation(deg_rows[chunk], ps[:, bank, :], ACT.Copy).then_inc(kept["deg"], 1)

            def encode():
                drain("xcT", head_dst(feat_1))
                keep_degrees(0, 7)
                act.wait_ge(in_w, 48)
                elu_parts("enc", BIAS_ENC)
                keep_degrees(1, 1)
                act.wait_ge(elu_done, 8)

            def late_emb():
                for k in range(4, 8):
                    act.wait_ge(full["emb"], k + 1)
                    act.activation(yh[:, 2 * k:2 * k + 2, :], ps[:, k, :].rearrange("p (b f) -> p b f", b=2), ACT.Copy)\
                        .then_inc(emb_late, 1)

            attention(1, 0, between=(encode, lambda: keep_degrees(2, 5), late_emb))
            attention(1, 1)
            drain("yT", head_dst(feat_1))
            elu_parts("yw", None)
            elu_parts("dec", BIAS_DEC)

            for t in range(NG + 2):
                if t < NG:
                    act.wait_ge(ln_shift_ready, t + 1)
                    for b in range(GB):
                        o = (b % 2) * F
                        ins = act.activation(x_now[:, GB * t + b, :], ps[:, 2 * t + b // 2, o:o + F], ACT.Identity,
                                             scale=ln_rs[:, t % 2, b:b + 1], bias=ln_shift[:, t % 2, b:b + 1])
                    ins.then_inc(ln_done, 1)
                for s in (1, 2, 0):
                    g = t - s
                    if 0 <= g < NG:
                        rows_g = slice(g * GB, (g + 1) * GB)
                        act.wait_ge(cut_rest[s], g + 1)
                        act.activation(parts[0][s][:, rows_g, :], rest[0][:, rows_g, :], ACT.Copy).then_inc(part_ready[s], 1)

            def drain_ax(layer):
                with act.Fori(0, NC) as m:
                    for c in range(FB):
                        act.wait_ge(full["ax"], FB * m + (8 * layer + c + 1))
                        if c == 0:
                            act.wait_ge(full["z"], 2 * m + (8 * layer + 2))
                        act.activation(ax_chunk[:, c, :], ps[:, c, :], ACT.Copy).then_inc(kept["ax"], 1)

            drain_ax(0)
            drain("x2T", [(feat_1[:, c, i * CH:(i + 1) * CH], ps[:, chunk_bank(i) + c, :])
                          for i in range(NC) for c in range(FB)])

            def softmax_exp(ib, b):
                act.wait_ge(max_ready, ib + 1)
                act.activation(prob[:, b, :], ps[:, 0:4, :], ACT.Exp, bias=neg_max[:, b:b + 1],
                               accum_out=row_sum[:, bass.ds(ib, 1)]).then_inc(p_ready, 1)

            def drains(ib, b):
                for q, bank in ((0, 4), (2, 6)):
                    act.wait_ge(t_full, 4 * ib + (q + 1))
                    act.activation(prob_t[:, b, q * BPC:(q + 1) * BPC, :],
                                   ps[:, bank, :].rearrange("p (k i) -> p k i", k=BPC),
                                   ACT.Copy).then_inc(t_act, 1)

            softmax_exp(0, 0)
            with act.Fori(0, NB // 2 - 1) as m:
                drains(2 * m, 0)
                softmax_exp(2 * m + 1, 1)
                drains(2 * m + 1, 1)
                softmax_exp(2 * m + 2, 0)
            drains(NB - 2, 0)
            softmax_exp(NB - 1, 1)
            drains(NB - 1, 1)

            drain_ax(1)

        @block.vector
        def _(v):
            steps = 0

            def step(ins):
                nonlocal steps
                steps += 1
                ins.then_inc(dve, 1)
                v.wait_ge(dve, steps)

            def wait_apart(sem_, count):
                v.wait_ge(sem_, count)
                v.memset(pause[:], 0.0)

            v.wait_ge(full["wv"], 1)
            v.wait_ge(in_h, 64)
            v.tensor_copy(wv0_s[:], ps[:, 7, :].rearrange("p (h e) -> p h e", h=H)).then_inc(kept["wv"], 1)
            v.wait_ge(full["wv"], 2)
            v.tensor_copy(wbd_x[:, :, P:P + 2], ps[:, 6, 0:4].rearrange("p (c e) -> p c e", c=FB)).then_inc(kept["wv"], 1)
            for b in range(NB):
                v.wait_ge(full["xw"], b + 1)
                src = ps[:, xw_bank(b), 0:FB * (P + 2)].rearrange("p (c e) -> p c e", c=FB)
                v.tensor_scalar(f2_half[:, b, :].rearrange("p (c e) -> p c e", c=FB), src[:, :, P:P + 2], 0.5, None,
                                ALU.mult).then_inc(f2_kept, 1)
                v.tensor_copy(yh[:, b, :].rearrange("p (c e) -> p c e", c=FB), src[:, :, 0:P]).then_inc(kept["xw"], 1)

            def mask_tile(ps_no, pair, m, k):
                g0 = PASS * ps_no + PAIR * pair
                row = adj_t[:, bass.ds(2 * m + k // 2, 1), :]
                if g0 == 0 and k % 2 == 0:
                    v.wait_ge(adj_in[k // 2], 16 * m + 16)
                    v.tensor_copy(row, adj_row[:, k // 2:k // 2 + 1, :]).then_inc(adj_cast, 1)
                    v.wait_ge(adj_cast, 2 * m + (k // 2 + 1))
                v.wait_ge(exp_done, 4 * m + (g0 + k + 1))
                tile = att_tile(ps_no, pair, m, k)
                for o in (0, N // 2):
                    v.tensor_tensor(tile[:, :, o:o + N // 2], tile[:, :, o:o + N // 2], row[:, :, o:o + N // 2],
                                    ALU.mult).then_inc(mask_done, 1)

            def mask(ps_no, pair, first=0):
                first_way = ps_no == 0 and pair == 0
                peel = first or first_way
                for k in range(first, 4 if peel else 0):
                    mask_tile(ps_no, pair, 0, k)
                    if first_way:
                        for n in (2 * k, 2 * k + 1):
                            v.wait_ge(full["f1"], 2 * NC + n + 1)
                            v.tensor_copy(f1[:, 2 + n // NC, (n % NC) * CH:(n % NC + 1) * CH], ps[:, 6 + n % 2, :])\
                                .then_inc(f1_late, 1)
                with v.Fori(1 if peel else 0, NB // 2) as m:
                    for k in range(4):
                        mask_tile(ps_no, pair, m, k)

            def take_head(ps_no, pair, h2):
                wid = D + 1
                h = 2 * pair + h2
                v.wait_ge(att_free, 4 + PASS * ps_no + PAIR * (pair + 1) - 1 + h2)
                groups = [(b3, PER_BANK * b3, min(NB - PER_BANK * b3, PER_BANK)) for b3 in range(HEAD_BANKS)]

                def acc(b3, cnt):
                    return ps[:, HEAD_BANKS * h2 + b3, 0:cnt * wid].rearrange("p (b e) -> p b e", e=wid)

                if ps_no == 0:
                    for b3, i0, cnt in groups:
                        ins = v.tensor_scalar(sums[:, h2, i0:i0 + cnt], acc(b3, cnt)[:, :, D], TINY, None, ALU.max)
                    step(ins)
                    step(v.reciprocal(rinv[:, h, :], sums[:, h2, :]))
                for b3, i0, cnt in groups:
                    ins = v.tensor_tensor(nodes[:, i0:i0 + cnt, h * D:(h + 1) * D], acc(b3, cnt)[:, :, 0:D],
                                          rinv[:, h, i0:i0 + cnt].unsqueeze(2).broadcast_to([P, cnt, D]), ALU.mult)
                ins.then_inc(acc_kept, 1)

            def change_pair(ps_no):
                take_head(ps_no, 0, 0)
                mask_tile(ps_no, 1, 0, 0)
                take_head(ps_no, 0, 1)

            pows = 0

            def bn_measure(buf, k, heads_first=False):
                c, i = divmod(k, NC) if heads_first else divmod(k, FB)[::-1]
                return v.bn_stats(bn_st[:, c, i, :], buf[:, c, i * CH:(i + 1) * CH])

            def batchnorm(buf, gain, shift, ins):
                nonlocal pows
                step(ins)
                for c in range(FB):
                    ins = v.bn_aggr(bn_mv[:, c, :], bn_st[:, c, :, :])
                step(ins)
                v.tensor_scalar(bn_ve[:], bn_mv[:, :, 1], EPS_BN, None, ALU.add).then_inc(var_ready, 1)
                pows += 1
                v.wait_ge(rstd_ready, pows)
                step(v.tensor_tensor(bn_a[:], bn_rs[:], par[:, gain, :], ALU.mult))
                for c in range(FB):
                    ins = v.scalar_tensor_tensor(bn_b[:, c:c + 1], bn_mv[:, c, 0:1], bn_a[:, c:c + 1],
                                                 par[:, shift, c:c + 1], ALU.mult, ALU.subtract)
                step(ins)
                for o in (0, N // 2):
                    for c in range(FB):
                        cols = buf[:, c, o:o + N // 2]
                        v.tensor_scalar(cols, cols, bn_a[:, c:c + 1], bn_b[:, c:c + 1], ALU.mult, ALU.subtract)\
                            .then_inc(bn_done, 1)

            elu_n = 0

            def elu_join(st, dst, residual, measure=False, heads_first=False):
                nonlocal elu_n
                for k in range(8):
                    c, i = divmod(k, NC) if heads_first else divmod(k, FB)[::-1]
                    cols = dst[:, c, i * CH:(i + 1) * CH]
                    v.wait_ge(elu_e, elu_n + 1)
                    v.wait_ge(kept[st], k + 1)
                    v.scalar_tensor_tensor(cols, e_tmp[:, elu_n % 2, :], 1.0, r_tmp[:, elu_n % 2, :], ALU.min,
                                           ALU.add).then_inc(elu_free, 1)
                    elu_n += 1
                    v.wait_ge(elu_free, elu_n)
                    if residual is not None:
                        ins = v.scalar_tensor_tensor(cols, cols, -1.0, residual[:, c, i * CH:(i + 1) * CH], ALU.add, ALU.add)
                    else:
                        ins = v.tensor_scalar(cols, cols, -1.0, None, ALU.add)
                    ins.then_inc(elu_done, 1)
                    if measure and k:
                        v.wait_ge(elu_done, elu_n - 1)
                        bn_measure(dst, k - 1)
                if measure:
                    v.wait_ge(elu_done, elu_n)
                    return bn_measure(dst, 7)

            def self_loops(op):
                for blocks in diagonal:
                    v.tensor_tensor(blocks, blocks, eye_b[:].unsqueeze(1).broadcast_to([P, blocks.shape[1], P]), op)\
                        .then_inc(loops_set, 1)

            def take_degrees(chunk, row):
                nonlocal pows
                row = row.rearrange("p (t i) -> p t i", i=P)
                step(v.tensor_tensor(row, row, ident[:].unsqueeze(1).broadcast_to([P, BPC, P]), ALU.mult))
                step(v.tensor_reduce(deg[:, chunk * BPC:(chunk + 1) * BPC], row, AX.X, ALU.add))
                for l, add in enumerate((1.0, EPS_DEG)):
                    v.tensor_scalar(deg_ve[:, l, chunk, :], deg[:, chunk * BPC:(chunk + 1) * BPC], add, None, ALU.add)\
                        .then_inc(var_ready, 1)
                    pows += 1

            mask(0, 0)
            change_pair(0)
            mask(0, 1, first=1)
            take_head(0, 1, 0)
            take_head(0, 1, 1)
            v.wait_ge(in_w, 48)
            for k in range(8):
                v.wait_ge(kept["xcT"], k + 1)
                last = bn_measure(feat_1, k, heads_first=True)
            batchnorm(feat_1, G_ENC, B_ENC, last)
            last = elu_join("enc", feat_2, feat_1, measure=True)
            batchnorm(feat_2, G_ENC2, B_ENC2, last)
            for k in range(4):
                v.wait_ge(full["emb"], k + 1)
                v.tensor_copy(yh[:, 2 * k:2 * k + 2, :], ps[:, k, :].rearrange("p (b f) -> p b f", b=2))\
                    .then_inc(kept["emb"], 1)
            for k in range(4):
                mask_tile(1, 0, 0, k)
            v.wait_ge(kept["deg"], NC - 1)
            for chunk in range(NC - 1):
                take_degrees(chunk, deg_rows[chunk])
            mask(1, 0, first=4)
            change_pair(1)
            for k in range(1, 4):
                mask_tile(1, 1, 0, k)
            v.wait_ge(full["deg"], NC - 1 + NB // 2)
            take_degrees(NC - 1, ps[:, 6, :])
            v.memset(pause[:], 0.0).then_inc(kept["deg"], 1)
            mask(1, 1, first=4)
            take_head(1, 1, 0)
            take_head(1, 1, 1)
            self_loops(ALU.add)
            elu_join("yw", feat_2, None, heads_first=True)
            last = elu_join("dec", feat_1, feat_2, measure=True)
            batchnorm(feat_1, G_DEC, B_DEC, last)

            def ln_measure(ln, g, slot):
                wait_apart(ln_stats, g + (NG * ln + 1))
                for t in range(GB):
                    ins = v.bn_aggr(ln_mv[:, slot, t, :], ln_st[:, slot, t, :])
                ins.then_inc(ln_aggr, 1)
                v.wait_ge(ln_aggr, g + (NG * ln + 1))
                v.tensor_scalar(ln_ve[:, slot, :], ln_mv[:, slot, :, 1], EPS_LN, None, ALU.add).then_inc(ln_var, 1)

            def ln_apply(ln, g, slot):
                v.wait_ge(ln_rstd, g + (NG * ln + 1))
                for t in range(GB):
                    row = x_now[:, bass.ds(GB * g + t, 1), :]
                    ins = v.tensor_scalar(row, row, ln_mv[:, slot, t, 0:1], ln_rs[:, slot, t:t + 1],
                                          ALU.subtract, ALU.mult)
                ins.then_inc(ln_done, 1)

            def cut_scale(cut, ln, g, rem):
                v.wait_ge(ln_done, g + (NG * ln + 1))
                v.tensor_tensor(rem, x_now[:, bass.ds(GB * g, GB), :],
                                dinv[:, cut, bass.ds(g, 1), :].rearrange("p a b -> p (a b)").unsqueeze(2).broadcast_to([P, GB, F]),
                                ALU.mult).then_inc(cut_rest[0], 1)

            def cut_less(cut, g, s, rem):
                v.wait_ge(part_ready[s - 1], g + (NG * cut + 1))
                v.tensor_tensor(rem, rem, parts[cut][s - 1][:, bass.ds(GB * g, GB), :], ALU.subtract).then_inc(cut_rest[s], 1)

            def l0_stats(g):
                v.wait_ge(full["l0"], 2 * g + 2)
                for b in range(GB):
                    o = (b % 2) * F
                    ins = v.bn_stats(ln_st[:, g % 2, b, :], ps[:, 2 * g + b // 2, o:o + F])
                ins.then_inc(ln_stats, 1)

            l0_stats(0)
            ln_measure(0, 0, 0)
            for t in range(NG + 2):
                if t < NG:
                    if t + 1 < NG:
                        l0_stats(t + 1)
                    v.wait_ge(ln_rstd, t + 1)
                    v.scalar_tensor_tensor(ln_shift[:, t % 2, :], ln_mv[:, t % 2, :, 0], -1.0, ln_rs[:, t % 2, :],
                                           ALU.mult, ALU.mult).then_inc(ln_shift_ready, 1)
                    if t + 1 < NG:
                        ln_measure(0, t + 1, (t + 1) % 2)
                for s in (1, 2):
                    g = t - s
                    if 0 <= g < NG:
                        cut_less(0, g, s, rest[0][:, g * GB:(g + 1) * GB, :])
                if t < NG:
                    cut_scale(0, 0, t, rest[0][:, t * GB:(t + 1) * GB, :])

            def gcn_tail(layer, ln):
                with v.Fori(0, NG) as g:
                    for k in range(2):
                        v.wait_ge(full["z"], 2 * g + (8 * layer + k + 3))
                        for t in (2 * k, 2 * k + 1):
                            z = ps[:, 2 + k:3 + k, (t % 2) * F:(t % 2) * F + F]
                            d = dinv[:, layer, bass.ds(g, 1), t]
                            if layer:
                                row = x_now[:, bass.ds(GB * g + t, 1), :]
                                ins = v.scalar_tensor_tensor(row, z, d, row, ALU.mult, ALU.add)
                            else:
                                row = nodes[:, bass.ds(GB * g + t, 1), :]
                                ins = v.tensor_scalar(row, z, d, 0.0, ALU.mult, ALU.max)
                        ins.then_inc(kept["z"], 1)
                        if layer:
                            wait_apart(kept["z"], 2 * g + (8 * layer + 2 + k + 1))
                        else:
                            v.wait_ge(kept["z"], 2 * g + (8 * layer + 2 + k + 1))
                            rows_k = x_now[:, bass.ds(GB * g + 2 * k, 2), :]
                            v.tensor_tensor(rows_k, rows_k, nodes[:, bass.ds(GB * g + 2 * k, 2), :], ALU.add)\
                                .then_inc(z_added, 1)
                            wait_apart(z_added, 2 * g + (k + 1))
                        for t in (2 * k, 2 * k + 1):
                            ins = v.bn_stats(ln_st[:, 0:1, t, :], x_now[:, bass.ds(GB * g + t, 1), :])
                    ins.then_inc(ln_stats, 1)
                    ln_measure(ln, g, 0)
                    ln_apply(ln, g, 0)

            gcn_tail(0, 1)
            self_loops(ALU.subtract)

            for k in range(16):
                i, c = divmod(k % 8, FB)
                dst = (feat_2 if k < 8 else feat_3)[:, c, i * CH:(i + 1) * CH]
                bank = chunk_bank(i) + c
                v.wait_ge(full["qk"], k + 1)
                if k < 8:
                    ins = v.tensor_scalar(dst, ps[:, bank, :], par[:, BIAS_Q, c:c + 1], 1.0 / 16, ALU.add, ALU.mult)
                else:
                    ins = v.tensor_scalar(dst, ps[:, bank, :], par[:, BIAS_K, c:c + 1], None, ALU.add)
                ins.then_inc(kept["qk"], 1)

            def keep_values(k):
                v.wait_ge(full["v"], k + 1)
                v.tensor_tensor(nodes[:, 2 * k:2 * k + 2, :], ps[:, 4 + k % 4, :].rearrange("p (b f) -> p b f", b=2),
                                row_s[:, 0:1, :].broadcast_to([P, 2, F]), ALU.add).then_inc(kept["v"], 1)

            def row_max(ib, b):
                v.wait_ge(s_full, ib + 1)
                v.tensor_reduce(neg_max[:, b:b + 1], ps[:, 0:4, :], AX.XY, ALU.max, negate=True).then_inc(max_ready, 1)

            def tail(ib, b):
                for q, bank in ((1, 5), (3, 4)):
                    v.wait_ge(t_full, 4 * ib + (q + 1))
                    v.tensor_copy(prob_t[:, b, q * BPC:(q + 1) * BPC, :],
                                  ps[:, bank, :].rearrange("p (k i) -> p k i", k=BPC)).then_inc(t_dve, 1)

            def finish(ib, t):
                v.wait_ge(p_ready, ib + 1)
                v.reciprocal(row_inv[:, bass.ds(ib, 1)], row_sum[:, bass.ds(ib, 1)]).then_inc(inv_ready, 1)
                v.wait_ge(o_full, ib + 1)
                v.wait_ge(inv_ready, ib + 1)
                v.scalar_tensor_tensor(x_now[:, bass.ds(ib, 1), :], ps[:, 7:8, 0:F], row_inv[:, bass.ds(ib, 1)],
                                       x_now[:, bass.ds(ib, 1), :], ALU.mult, ALU.add).then_inc(o_kept, 1)
                wait_apart(o_kept, ib + 1)
                ins = v.bn_stats(ln_st[:, 0:1, t, :], x_now[:, bass.ds(ib, 1), :])
                if t == GB - 1:
                    ins.then_inc(ln_stats, 1)

            def attend_group(g):
                for t in range(GB):
                    tail(GB * g + t, t % 2)
                    if not (isinstance(g, int) and t == GB - 1):
                        row_max(GB * g + (t + 1), (t + 1) % 2)
                    finish(GB * g + t, t)
                ln_measure(2, g, 0)
                ln_apply(2, g, 0)
                cut_scale(1, 2, g, rest[1])
                for s in range(3):
                    if s:
                        cut_less(1, g, s, rest[1])
                    v.wait_ge(cut_rest[s], g + (NG + 1))
                    v.tensor_copy(parts[1][s][:, bass.ds(GB * g, GB), :], rest[1]).then_inc(part_ready[s], 1)

            for k in range(4):
                keep_values(k)
            row_max(0, 0)
            for k in range(4, 8):
                keep_values(k)
            with v.Fori(0, NG - 1) as g:
                attend_group(g)
            attend_group(NG - 1)
            for g in range(NG):
                rows_g = x_now[:, g * GB:(g + 1) * GB, :]
                v.tensor_tensor(rows_g, rows_g, row_s[:, 1:2, :].broadcast_to([P, GB, F]), ALU.add).then_inc(biased, 1)
            v.wait_ge(biased, NG)
            gcn_tail(1, 3)

        @block.tensor
        def _(pe):
            def feature_product(st, w, src, first=lambda k: None):
                for i in range(NC):
                    for e in range(FB):
                        k = i * FB + e
                        first(k)
                        for f in range(FB):
                            mm = pe.matmul(ps[:, k, :], w_all[:, w, f, e * P:(e + 1) * P],
                                           src[:, f, i * CH:(i + 1) * CH], start=f == 0, stop=f == FB - 1)
                        mm.then_inc(full[st], 1)

            def heads_to_features(st, ps_no):
                for c in range(FB):
                    for i in range(NC):
                        k = c * NC + i
                        pe.wait_ge(acc_kept, 4 * ps_no + (3 if k < HEAD_BANKS else 4))
                        if ps_no and k == 6:
                            pe.wait_ge(kept["deg"], NC)
                        for t in range(BPC):
                            mm = pe.transpose(ps[:, k, t * P:(t + 1) * P],
                                              nodes[:, i * BPC + t, c * P:(c + 1) * P], ident[:])
                        mm.then_inc(full[st], 1)

            def to_nodes(st, src, first=lambda k: None):
                for k in range(8):
                    first(k)
                    for b in (2 * k, 2 * k + 1):
                        for c in range(FB):
                            mm = pe.transpose(ps[:, k, (b % 2) * F + c * P:(b % 2) * F + (c + 1) * P],
                                              src[:, c, b * P:(b + 1) * P], ident[:])
                    mm.then_inc(full[st], 1)

            def keep_warm(bank, products, free=True):
                for _ in range(products):
                    pe.matmul(ps[:, bank, :], zeros_b[:, 0:P], zeros_b[:], start=free, stop=free, skip_group_check=True)

            pe.wait_ge(consts, 1)
            keep_warm(0, 6)
            pe.wait_ge(in_h, 64)
            for h in range(H):
                mm = pe.matmul(ps[:, 7, h * P:(h + 1) * P], wtbd_s[:, h // 2, :], v0_s[:, h, :], start=True, stop=True)
            mm.then_inc(full["wv"], 1)
            for c in range(FB):
                mm = pe.matmul(ps[:, 6, 2 * c:2 * c + 2], wtbd_s[:, c, :], v1_s[:, c, :], start=True, stop=True)
            mm.then_inc(full["wv"], 1)
            keep_warm(0, 12)
            pe.wait_ge(in_x, 32)

            def f1_chunk(h, i, bank):
                pe.matmul(ps[:, bank, :], wv0_s[:, h, :], x_t[:, h // 2, i * CH:(i + 1) * CH],
                          start=True, stop=True).then_inc(full["f1"], 1)

            def xw_block(b):
                if b > 4:
                    pe.wait_ge(kept["xw"], b - 3)
                elif b:
                    pe.wait_ge(kept["f1"], b % 4 + 1)
                for c in range(FB):
                    mm = pe.matmul(ps[:, xw_bank(b), c * (P + 2):(c + 1) * (P + 2)], x_t[:, c, b * P:(b + 1) * P],
                                   wbd_x[:, c, :], start=True, stop=True)
                mm.then_inc(full["xw"], 1)

            pe.wait_ge(kept["wv"], 2)
            xw_block(0)
            for i in range(NC):
                f1_chunk(0, i, i)
            pe.wait_ge(kept["xw"], 1)
            for i in range(NC):
                f1_chunk(1, i, 4 + i)
            for b in range(1, NB):
                xw_block(b)

            def degree_products(chunk, bank, blocks):
                whole = len(blocks) == NB
                for j in blocks:
                    mm = pe.matmul(ps[:, bank, :], ones_b[:], adj_t[:, bass.ds(j, 1), chunk * CH:(chunk + 1) * CH],
                                   start=whole and j == 0, stop=not whole or j == NB - 1, skip_group_check=True)
                mm.then_inc(full["deg"], 1)

            def attend(ps_no, pair):
                wid = D + 1
                g0 = PASS * ps_no + PAIR * pair

                def open_banks(banks):
                    for b in banks:
                        pe.matmul(ps[:, b, :], zeros_b[:, 0:P], zeros_b[:], start=True, stop=True, skip_group_check=True)

                def tile(m, k):
                    pe.wait_ge(mov_ready, 4 * m + (g0 + k + 1))
                    for b in range(NB):
                        if b % (NB // 2) == 0:
                            pe.wait_ge(mask_done, 8 * m + (2 * (g0 + k) + b // (NB // 2) + 1))
                        o = (b % PER_BANK) * wid
                        mm = pe.matmul(ps[:, HEAD_BANKS * (k % 2) + b // PER_BANK, o:o + MOVING],
                                       att_tile(ps_no, pair, m, k)[:, :, b * P:(b + 1) * P], mov_s[:, k, :],
                                       start=False, stop=True, skip_group_check=True)
                    mm.then_inc(att_free, 1)

                for k in range(4):
                    if not g0 and k == 0:
                        pe.wait_ge(kept["xw"], NB)
                        pe.wait_ge(kept["f1"], 2 * NC)
                    if k < 2:
                        if g0:
                            pe.wait_ge(acc_kept, 2 * (2 * ps_no + pair - 1) + k + 1)
                        open_banks(range(HEAD_BANKS * k, HEAD_BANKS * (k + 1)))
                    if not g0:
                        for n in (2 * k, 2 * k + 1):
                            if k:
                                pe.wait_ge(f1_late, n - 1)
                            f1_chunk(2 + n // NC, n % NC, 6 + n % 2)
                    tile(0, k)
                last_degrees = ps_no and not pair
                if last_degrees:
                    open_banks((6,))
                    degree_products(NC - 1, 6, (0, 1))
                with pe.Fori(1, NB // 2) as m:
                    for k in range(4):
                        tile(m, k)
                    if last_degrees:
                        degree_products(NC - 1, 6, (2 * m, 2 * m + 1))

            pe.wait_ge(consts, 6)
            attend(0, 0)
            attend(0, 1)
            heads_to_features("xcT", 0)
            pe.wait_ge(in_w, 48)
            pe.wait_ge(kept["xcT"], 8)
            degree_products(0, 7, range(NB))
            keep_warm(0, 6)

            def enc_ready(k):
                pe.wait_ge(bn_done, 2 * (k // 4) + 2)
                if k == 7:
                    pe.wait_ge(kept["deg"], 1)

            feature_product("enc", W_ENC, feat_1, first=enc_ready)

            def emb_ready(k):
                pe.wait_ge(bn_done, 4 + 2 * (k // 4) + 2)
                pe.wait_ge(kept["enc"], k + 1)
                if k in (1, 5):
                    pe.wait_ge(kept["deg"], 2 + k // 5)

            pe.wait_ge(kept["enc"], 6)
            degree_products(1, 1, range(NB))
            degree_products(2, 5, range(NB))
            keep_warm(0, 4)
            to_nodes("emb", feat_2, first=emb_ready)
            pe.wait_ge(kept["emb"], 4)
            pe.wait_ge(emb_late, 4)
            attend(1, 0)
            attend(1, 1)
            heads_to_features("yT", 1)
            for c in range(FB):
                for i in range(NC):
                    pe.wait_ge(kept["yT"], c * NC + i + 1)
                    pe.matmul(ps[:, c * NC + i, :], wtbd_s[:, c, :], feat_1[:, c, i * CH:(i + 1) * CH],
                              start=True, stop=True).then_inc(full["yw"], 1)

            def dec_ready(k):
                pe.wait_ge(kept["yw"], k + 1)
                pe.wait_ge(elu_done, 8 + NC + k // FB + 1)

            feature_product("dec", W_DEC, feat_2, first=dec_ready)
            pe.wait_ge(in_res, 16)
            for k in range(8):
                pe.wait_ge(kept["dec"], k + 1)
                pe.matmul(ps[:, k, :], ident[:], x_now[:, 2 * k:2 * k + 2, :], start=True, stop=False,
                          skip_group_check=True)
            keep_warm(0, 8, free=False)
            for k in range(8):
                pe.wait_ge(bn_done, 8 + 2 * (k // 4) + 2)
                for b in (2 * k, 2 * k + 1):
                    for c in range(FB):
                        o = (b % 2) * F + c * P
                        mm = pe.matmul(ps[:, k, o:o + P], feat_1[:, c, b * P:(b + 1) * P], ident[:],
                                       start=False, stop=True, skip_group_check=True)
                mm.then_inc(full["l0"], 1)

            def gcn(layer, w):
                def ax_part(m, c, s, j):
                    return pe.matmul(ps[:, c, :], parts[layer][s][:, j, c * P:(c + 1) * P],
                                     adj_t[:, j, bass.ds(m * CH, CH)], start=s == 0 and j == 0,
                                     stop=j == NB - 1 and s == 2, skip_group_check=True)

                def ax(m, c):
                    pe.wait_ge(kept["ax"], FB * m + (8 * layer + c + 1))
                    for s in range(3):
                        for j in range(NB):
                            mm = ax_part(m, c, s, j)
                    mm.then_inc(full["ax"], 1)

                def z(m):
                    pe.wait_ge(kept["ax"], FB * m + (8 * layer + 2 + 2))
                    for k in range(2):
                        pe.wait_ge(kept["z"], 2 * m + (8 * layer + k + 1))
                        for b in (2 * k, 2 * k + 1):
                            for f in range(FB):
                                mm = pe.matmul(ps[:, 2 + k, (b % 2) * F:(b % 2) * F + F], ax_chunk[:, f, b * P:(b + 1) * P],
                                               w_all[:, w, f, :], start=f == 0, stop=f == FB - 1)
                        mm.then_inc(full["z"], 1)

                pe.wait_ge(kept["ax"], 8 * layer + 2)
                order = [(g, s) for g in range(NG) for s in range(3)]
                if layer == 0:
                    order.sort(key=lambda gs: gs[0] + gs[1])
                for g, s in order:
                    pe.wait_ge(part_ready[s], NG * layer + g + 1)
                    for c in range(FB):
                        for j in range(g * GB, (g + 1) * GB):
                            mm = ax_part(0, c, s, j)
                        if (g, s) == order[-1]:
                            mm.then_inc(full["ax"], 1)
                with pe.Fori(0, NC - 1) as m:
                    ax(m + 1, 0)
                    z(m)
                    ax(m + 1, 1)
                z(NC - 1)

            pe.wait_ge(ln_done, 1)
            pe.wait_ge(loops_set, 2)
            gcn(0, W_L1)

            def x2_chunk(i):
                pe.wait_ge(ln_done, NG + i + 1)
                for c in range(FB):
                    for t in range(BPC):
                        mm = pe.transpose(ps[:, chunk_bank(i) + c, t * P:(t + 1) * P],
                                          x_now[:, i * BPC + t, c * P:(c + 1) * P], ident[:])
                    mm.then_inc(full["x2T"], 1)

            def qk_chunk(w, i, first):
                for e in range(FB):
                    first(i * FB + e)
                    for f in range(FB):
                        mm = pe.matmul(ps[:, chunk_bank(i) + e, :], w_all[:, w, f, e * P:(e + 1) * P],
                                       feat_1[:, f, i * CH:(i + 1) * CH], start=f == 0, stop=f == FB - 1)
                    mm.then_inc(full["qk"], 1)

            def value_blocks(ks):
                for k in ks:
                    if k < 4:
                        pe.wait_ge(kept["qk"], 8 + k + 1)
                    else:
                        pe.wait_ge(kept["v"], k - 3)
                    for b in (2 * k, 2 * k + 1):
                        for f in range(FB):
                            mm = pe.matmul(ps[:, 4 + k % 4, (b % 2) * F:(b % 2) * F + F], feat_1[:, f, b * P:(b + 1) * P],
                                           w_all[:, W_V, f, :], start=f == 0, stop=f == FB - 1)
                    mm.then_inc(full["v"], 1)

            for i in range(NC - 1):
                x2_chunk(i)
            for i in range(NC - 1):
                qk_chunk(W_Q, i, lambda k: pe.wait_ge(kept["x2T"], FB * (k // FB + 1)))
            x2_chunk(NC - 1)
            qk_chunk(W_Q, NC - 1, lambda k: pe.wait_ge(kept["x2T"], 8))
            for i in range(NC):
                qk_chunk(W_K, i, lambda k: pe.wait_ge(kept["qk"], k + 1))

            def scores(ib, b, free):
                pe.wait_ge(q_ready, ib + 1)
                if free:
                    pe.wait_ge(p_ready, ib)
                for jc in range(NC):
                    for f in range(FB):
                        pe.matmul(ps[:, jc, :], q_blk[:, b, f, :], feat_3[:, f, jc * CH:(jc + 1) * CH],
                                  start=f == 0, stop=False, skip_group_check=True)
                    for t in range(BPC):
                        mm = pe.matmul(ps[:, jc, t * P:(t + 1) * P], adj_t[:, jc * BPC + t, bass.ds(ib * P, P)],
                                       two_b[:], start=False, stop=True, skip_group_check=True)
                mm.then_inc(s_full, 1)

            def values(ib, b, first=False):
                pe.wait_ge(p_ready, ib + 1)
                for q, bank in enumerate((4, 5, 6, 4)):
                    if q == 3:
                        pe.wait_ge(t_act, 2 * ib + 1)
                    elif not first:
                        if q == 1:
                            pe.wait_ge(t_dve, 2 * ib - 1)
                        elif q == 0:
                            pe.wait_ge(t_dve, 2 * ib)
                        else:
                            pe.wait_ge(t_act, 2 * ib)
                    for t in range(BPC):
                        j = q * BPC + t
                        mm = pe.transpose(ps[:, bank, t * P:(t + 1) * P], prob[:, b, j * P:(j + 1) * P], ident[:])
                    mm.then_inc(t_full, 1)
                if not first:
                    pe.wait_ge(o_kept, ib)
                for q in range(NC):
                    pe.wait_ge(t_act if q % 2 == 0 else t_dve, 2 * ib + (q // 2 + 1))
                    for t in range(BPC):
                        j = q * BPC + t
                        mm = pe.matmul(ps[:, 7, 0:F], prob_t[:, b, j, :], nodes[:, j, :],
                                       start=j == 0, stop=j == NB - 1)
                mm.then_inc(o_full, 1)

            value_blocks(range(4))
            pe.wait_ge(kept["qk"], 16)
            pe.wait_ge(loops_set, 4)
            scores(0, 0, False)
            value_blocks(range(4, 8))
            scores(1, 1, True)
            pe.wait_ge(kept["v"], 8)
            values(0, 0, first=True)
            with pe.Fori(0, NB // 2 - 1) as m:
                scores(2 * m + 2, 0, True)
                values(2 * m + 1, 1)
                scores(2 * m + 3, 1, True)
                values(2 * m + 2, 0)
            values(NB - 1, 1)

            pe.wait_ge(o_kept, NB)
            gcn(1, W_L3)


def kernel(x, adj, L0_gnn_W, L0_gnn_V, L0_gnn_enc_bn_gamma, L0_gnn_enc_bn_beta, L0_gnn_enc_mlp_W,
           L0_gnn_enc_mlp_b, L0_gnn_enc_mlp_bn_gamma, L0_gnn_enc_mlp_bn_beta, L0_gnn_dec_mlp_W,
           L0_gnn_dec_mlp_b, L0_gnn_dec_mlp_bn_gamma, L0_gnn_dec_mlp_bn_beta, L1_gnn_W,
           L2_gnn_Wq, L2_gnn_bq, L2_gnn_Wk, L2_gnn_bk, L2_gnn_Wv, L2_gnn_bv, L3_gnn_W, L3_gnn_b):
    import numpy as np
    import concourse.bacc as bacc
    from concourse.bass_utils import run_bass_kernel_spmd

    W, V = np.asarray(L0_gnn_W), np.asarray(L0_gnn_V)
    wbd = np.zeros((FB, P, P), W.dtype)
    wtbd = np.zeros((FB, P, P), W.dtype)
    v0rep = np.zeros((H, P, P), V.dtype)
    v1 = np.zeros((FB, P, 2), V.dtype)
    for h in range(H):
        c, r = divmod(h, 2)
        rows = slice(r * D, (r + 1) * D)
        wbd[c, rows, rows] = W[h]
        wtbd[c, rows, rows] = W[h].T
        v0rep[h, rows, :] = V[h, 0]
        v1[c, rows, r] = V[h, 1, :, 0]

    def blocks(w):
        return np.asarray(w).reshape(FB, P, F).transpose(1, 0, 2)

    weights = np.stack([blocks(np.asarray(L0_gnn_enc_mlp_W).T), blocks(np.asarray(L0_gnn_dec_mlp_W).T),
                        blocks(L1_gnn_W), blocks(L2_gnn_Wq), blocks(L2_gnn_Wk), blocks(L2_gnn_Wv),
                        blocks(np.asarray(L3_gnn_W).T)], axis=1)
    params = np.stack([np.asarray(a).reshape(FB, P).T for a in (
        L0_gnn_enc_bn_gamma, L0_gnn_enc_bn_beta, L0_gnn_enc_mlp_b, L0_gnn_enc_mlp_bn_gamma,
        L0_gnn_enc_mlp_bn_beta, L0_gnn_dec_mlp_b, L0_gnn_dec_mlp_bn_gamma, L0_gnn_dec_mlp_bn_beta,
        L2_gnn_bq, L2_gnn_bk)], axis=1)
    rows = np.stack([np.broadcast_to(np.asarray(a), (P, F)) for a in (L2_gnn_bv, L3_gnn_b)], axis=1)
    x, adj = np.asarray(x), np.asarray(adj)
    arrays = {k: np.ascontiguousarray(a) for k, a in dict(
        x=x, xT=x.T, adjT=adj.T, wbd=wbd, wtbd=wtbd, v0rep=v0rep, v1=v1, weights=weights,
        params=params, rows=rows).items()}

    nc = bacc.Bacc("TRN2", target_bir_lowering=False, num_devices=1)
    aps = {k: nc.dram_tensor("in_" + k, a.shape, mybir.dt.from_np(a.dtype), kind="ExternalInput").ap()
           for k, a in arrays.items()}
    out = nc.dram_tensor("out", (N, F), F32, kind="ExternalOutput").ap()
    gnn_stack(nc, out=out, **aps)
    r = run_bass_kernel_spmd(nc, [{"in_" + k: a for k, a in arrays.items()}], core_ids=[0])
    return r.results[0]["out"]
```
